# Optimizing a Trainium2 kernel written in Bass

```python
import numpy as np
import jax
import jax.numpy as jnp

def _softmax(x, axis=-1):
    return jax.nn.softmax(x, axis=axis)
def _gelu(x):
    return jax.nn.gelu(x, approximate=True)
def _silu(x):
    return jax.nn.silu(x)
def _sigmoid(x):
    return jax.nn.sigmoid(x)
def _layernorm(x, axis=-1, eps=1e-5):
    m = jnp.mean(x, axis=axis, keepdims=True)
    v = jnp.var(x, axis=axis, keepdims=True)
    return (x - m) / jnp.sqrt(v + eps)
def _scatter_add(tgt, idx, src, axis=0):
    return tgt.at[idx].add(src)
def _segment_sum(src, seg, n):
    return jax.ops.segment_sum(src, seg, n)

kernel_name = 'mk_conv_seq_d2_conv_nchw256_44d5bb'

def setup_inputs(seed: int = 0):
    np.random.seed(seed)
    _w = jnp.asarray
    def _rec_inputs():
        import jax
        import jax.numpy as jnp
        _gk = jax.random.key(seed)
        x = -0.0002928 + 1 * jax.random.normal(jax.random.fold_in(_gk, 1), (4, 256, 64, 64), jnp.float32)
        return x
    x = _rec_inputs()
    def _L0_conv_setup():
        import jax, jax.numpy as jnp
        import numpy as np
        C = 256
        D = C // 8
        B, H, W = (4, 64, 64)
        key = jax.random.key(seed)
        ks = jax.random.split(key, 8)
        inp = {'x': jax.random.normal(ks[0], (B, C, H, W), dtype=jnp.float32), 'wq': jax.random.normal(ks[1], (D, C), dtype=jnp.float32) * (1.0 / np.sqrt(C)), 'bq': jax.random.normal(ks[2], (D,), dtype=jnp.float32) * 0.02, 'wk': jax.random.normal(ks[3], (D, C), dtype=jnp.float32) * (1.0 / np.sqrt(C)), 'bk': jax.random.normal(ks[4], (D,), dtype=jnp.float32) * 0.02, 'wv': jax.random.normal(ks[5], (C, C), dtype=jnp.float32) * (1.0 / np.sqrt(C)), 'bv': jax.random.normal(ks[6], (C,), dtype=jnp.float32) * 0.02, 'gamma': jax.random.normal(ks[7], (1,), dtype=jnp.float32)}
        return inp
    _L0_conv_all = _L0_conv_setup()
    _L0_conv_in = {k: v for k, v in _L0_conv_all.items() if k in ('wq', 'bq', 'wk', 'bk', 'wv', 'bv', 'gamma', )}
    del _L0_conv_all

    def _L1_conv_setup():
        import jax, jax.numpy as jnp
        import numpy as np
        D_MODEL = 256
        D_STATE = 128
        D_CONV = 4
        HEADDIM = 64
        NHEADS = D_MODEL // HEADDIM
        D_INNER = D_MODEL
        CONV_DIM = D_INNER + 2 * D_STATE
        D_IN_PROJ = 2 * D_INNER + 2 * D_STATE + NHEADS
        EPS = 1e-05

        def _mamba2_core(u, in_w, conv_w, conv_b, dt_bias, A_log, Dp, rms_w, out_w):
            b, L, _ = u.shape
            zxbcdt = jnp.einsum('bld,ed->ble', u, in_w)
            z = zxbcdt[..., :D_INNER]
            xBC = zxbcdt[..., D_INNER:D_INNER + CONV_DIM]
            dt = jax.nn.softplus(zxbcdt[..., -NHEADS:] + dt_bias)
            xc = jax.lax.conv_general_dilated(xBC.transpose(0, 2, 1), conv_w[:, None, :], (1,), [(D_CONV - 1, 0)], dimension_numbers=('NCH', 'OIH', 'NCH'), feature_group_count=CONV_DIM)
            xBC = jax.nn.silu((xc + conv_b[None, :, None]).transpose(0, 2, 1))
            xs = xBC[..., :D_INNER].reshape(b, L, NHEADS, HEADDIM)
            Bm = xBC[..., D_INNER:D_INNER + D_STATE]
            Cm = xBC[..., D_INNER + D_STATE:]
            A = -jnp.exp(A_log)

            def step(state, inp):
                dt_t, x_t, B_t, C_t = inp
                dA = jnp.exp(dt_t * A)
                state = state * dA[:, :, None, None] + (dt_t[:, :, None] * x_t)[..., None] * B_t[:, None, None, :]
                y_t = jnp.einsum('bhpn,bn->bhp', state, C_t)
                return (state, y_t)
            state0 = jnp.zeros((b, NHEADS, HEADDIM, D_STATE), u.dtype)
            _, ys = jax.lax.scan(step, state0, (dt.transpose(1, 0, 2), xs.transpose(1, 0, 2, 3), Bm.transpose(1, 0, 2), Cm.transpose(1, 0, 2)))
            y = ys.transpose(1, 0, 2, 3) + Dp[None, None, :, None] * xs
            y = y.reshape(b, L, D_INNER)
            y = y * jax.nn.silu(z)
            y = y * jax.lax.rsqrt(jnp.mean(y * y, axis=-1, keepdims=True) + EPS) * rms_w
            return jnp.einsum('bld,ed->ble', y, out_w)
        key = jax.random.key(seed)
        ks = jax.random.split(key, 12)
        b, h, w = (4, 32, 32)
        x = jax.random.normal(ks[0], (b, D_MODEL, h, w), jnp.float32)
        s = 0.02
        params = {'norm_g': jnp.ones((D_MODEL,), jnp.float32), 'norm_b': jnp.zeros((D_MODEL,), jnp.float32), 'in_w': jax.random.normal(ks[1], (D_IN_PROJ, D_MODEL), jnp.float32) * s, 'conv_w': jax.random.normal(ks[2], (CONV_DIM, D_CONV), jnp.float32) * 0.1, 'conv_b': jnp.zeros((CONV_DIM,), jnp.float32), 'dt_bias': jax.random.normal(ks[3], (NHEADS,), jnp.float32) * 0.1, 'A_log': jnp.log(jax.random.uniform(ks[4], (NHEADS,), jnp.float32, 1.0, 16.0)), 'Dp': jnp.ones((NHEADS,), jnp.float32), 'rms_w': jnp.ones((D_INNER,), jnp.float32), 'out_w': jax.random.normal(ks[5], (D_MODEL, D_INNER), jnp.float32) * s, 'se1_w': jax.random.normal(ks[6], (D_MODEL // 4, D_MODEL), jnp.float32) * s, 'se1_b': jnp.zeros((D_MODEL // 4,), jnp.float32), 'se2_w': jax.random.normal(ks[7], (D_MODEL, D_MODEL // 4), jnp.float32) * s, 'se2_b': jnp.zeros((D_MODEL,), jnp.float32)}
        return {'x': x, **params}
    _L1_conv_all = _L1_conv_setup()
    _L1_conv_in = {k: v for k, v in _L1_conv_all.items() if k in ('norm_g', 'norm_b', 'in_w', 'conv_w', 'conv_b', 'dt_bias', 'A_log', 'Dp', 'rms_w', 'out_w', 'se1_w', 'se1_b', 'se2_w', 'se2_b', )}
    del _L1_conv_all

    return {
        "x": x,
        "L0_conv_wq": _L0_conv_in["wq"],
        "L0_conv_bq": _L0_conv_in["bq"],
        "L0_conv_wk": _L0_conv_in["wk"],
        "L0_conv_bk": _L0_conv_in["bk"],
        "L0_conv_wv": _L0_conv_in["wv"],
        "L0_conv_bv": _L0_conv_in["bv"],
        "L0_conv_gamma": _L0_conv_in["gamma"],
        "L1_conv_norm_g": _L1_conv_in["norm_g"],
        "L1_conv_norm_b": _L1_conv_in["norm_b"],
        "L1_conv_in_w": _L1_conv_in["in_w"],
        "L1_conv_conv_w": _L1_conv_in["conv_w"],
        "L1_conv_conv_b": _L1_conv_in["conv_b"],
        "L1_conv_dt_bias": _L1_conv_in["dt_bias"],
        "L1_conv_A_log": _L1_conv_in["A_log"],
        "L1_conv_Dp": _L1_conv_in["Dp"],
        "L1_conv_rms_w": _L1_conv_in["rms_w"],
        "L1_conv_out_w": _L1_conv_in["out_w"],
        "L1_conv_se1_w": _L1_conv_in["se1_w"],
        "L1_conv_se1_b": _L1_conv_in["se1_b"],
        "L1_conv_se2_w": _L1_conv_in["se2_w"],
        "L1_conv_se2_b": _L1_conv_in["se2_b"],
    }

def reference(x, L0_conv_wq, L0_conv_bq, L0_conv_wk, L0_conv_bk, L0_conv_wv, L0_conv_bv, L0_conv_gamma, L1_conv_norm_g, L1_conv_norm_b, L1_conv_in_w, L1_conv_conv_w, L1_conv_conv_b, L1_conv_dt_bias, L1_conv_A_log, L1_conv_Dp, L1_conv_rms_w, L1_conv_out_w, L1_conv_se1_w, L1_conv_se1_b, L1_conv_se2_w, L1_conv_se2_b):
    import jax
    import jax.numpy as jnp
    def _L0_conv_ref(x, wq, bq, wk, bk, wv, bv, gamma):
        import jax, jax.numpy as jnp
        import numpy as np
        C = 256
        D = C // 8
        B, H, W = (4, 64, 64)
        b, c, h, w = x.shape
        n = h * w
        xf = x.reshape(b, c, n)
        q = jnp.einsum('dc,bcn->bnd', wq, xf) + bq
        k = jnp.einsum('dc,bcn->bdn', wk, xf) + bk[:, None]
        energy = jnp.einsum('bnd,bdm->bnm', q, k)
        attn = jax.nn.softmax(energy, axis=-1)
        v = jnp.einsum('dc,bcn->bdn', wv, xf) + bv[:, None]
        out = jnp.einsum('bcn,bmn->bcm', v, attn).reshape(b, c, h, w)
        return gamma * out + x

    def _L1_conv_ref(x, norm_g, norm_b, in_w, conv_w, conv_b, dt_bias, A_log, Dp, rms_w, out_w, se1_w, se1_b, se2_w, se2_b):
        import jax, jax.numpy as jnp
        import numpy as np
        D_MODEL = 256
        D_STATE = 128
        D_CONV = 4
        HEADDIM = 64
        NHEADS = D_MODEL // HEADDIM
        D_INNER = D_MODEL
        CONV_DIM = D_INNER + 2 * D_STATE
        D_IN_PROJ = 2 * D_INNER + 2 * D_STATE + NHEADS
        EPS = 1e-05

        def _mamba2_core(u, in_w, conv_w, conv_b, dt_bias, A_log, Dp, rms_w, out_w):
            b, L, _ = u.shape
            zxbcdt = jnp.einsum('bld,ed->ble', u, in_w)
            z = zxbcdt[..., :D_INNER]
            xBC = zxbcdt[..., D_INNER:D_INNER + CONV_DIM]
            dt = jax.nn.softplus(zxbcdt[..., -NHEADS:] + dt_bias)
            xc = jax.lax.conv_general_dilated(xBC.transpose(0, 2, 1), conv_w[:, None, :], (1,), [(D_CONV - 1, 0)], dimension_numbers=('NCH', 'OIH', 'NCH'), feature_group_count=CONV_DIM)
            xBC = jax.nn.silu((xc + conv_b[None, :, None]).transpose(0, 2, 1))
            xs = xBC[..., :D_INNER].reshape(b, L, NHEADS, HEADDIM)
            Bm = xBC[..., D_INNER:D_INNER + D_STATE]
            Cm = xBC[..., D_INNER + D_STATE:]
            A = -jnp.exp(A_log)

            def step(state, inp):
                dt_t, x_t, B_t, C_t = inp
                dA = jnp.exp(dt_t * A)
                state = state * dA[:, :, None, None] + (dt_t[:, :, None] * x_t)[..., None] * B_t[:, None, None, :]
                y_t = jnp.einsum('bhpn,bn->bhp', state, C_t)
                return (state, y_t)
            state0 = jnp.zeros((b, NHEADS, HEADDIM, D_STATE), u.dtype)
            _, ys = jax.lax.scan(step, state0, (dt.transpose(1, 0, 2), xs.transpose(1, 0, 2, 3), Bm.transpose(1, 0, 2), Cm.transpose(1, 0, 2)))
            y = ys.transpose(1, 0, 2, 3) + Dp[None, None, :, None] * xs
            y = y.reshape(b, L, D_INNER)
            y = y * jax.nn.silu(z)
            y = y * jax.lax.rsqrt(jnp.mean(y * y, axis=-1, keepdims=True) + EPS) * rms_w
            return jnp.einsum('bld,ed->ble', y, out_w)
        b, c, h, w = x.shape
        L = h * w
        u = x.transpose(0, 2, 3, 1).reshape(b, L, c)
        mu = jnp.mean(u, axis=-1, keepdims=True)
        var = jnp.mean((u - mu) ** 2, axis=-1, keepdims=True)
        u = (u - mu) * jax.lax.rsqrt(var + EPS) * norm_g + norm_b
        out = _mamba2_core(u, in_w, conv_w, conv_b, dt_bias, A_log, Dp, rms_w, out_w)
        out_img = out.reshape(b, h, w, c).transpose(0, 3, 1, 2)
        pooled = jnp.mean(out_img, axis=(2, 3))
        hdn = jax.nn.relu(pooled @ se1_w.T + se1_b)
        attn = jax.nn.sigmoid(hdn @ se2_w.T + se2_b)
        return x + out_img * attn[:, :, None, None]

    def _gn(v, G=32, eps=1e-5):
        B_, C_, H_, W_ = v.shape
        g = v.reshape(B_, G, C_ // G, H_, W_)
        m = jnp.mean(g, axis=(2, 3, 4), keepdims=True)
        s = jnp.var(g, axis=(2, 3, 4), keepdims=True)
        return ((g - m) / jnp.sqrt(s + eps)).reshape(v.shape)

    def _ln_c(v, eps=1e-6):
        m = jnp.mean(v, axis=1, keepdims=True)
        s = jnp.var(v, axis=1, keepdims=True)
        return (v - m) / jnp.sqrt(s + eps)

    def _ln_t(v, eps=1e-5):
        m = jnp.mean(v, axis=-1, keepdims=True)
        s = jnp.var(v, axis=-1, keepdims=True)
        return (v - m) / jnp.sqrt(s + eps)

    def _to_tokens(v):
        B_, C_, H_, W_ = v.shape
        return v.reshape(B_, C_, H_ * W_).transpose(0, 2, 1)
    def _from_tokens(t, like):
        B_, C_, H_, W_ = like.shape
        return t.transpose(0, 2, 1).reshape(B_, C_, H_, W_)

    x = _L0_conv_ref(x, L0_conv_wq, L0_conv_bq, L0_conv_wk, L0_conv_bk, L0_conv_wv, L0_conv_bv, L0_conv_gamma)
    x = _L1_conv_ref(x, L1_conv_norm_g, L1_conv_norm_b, L1_conv_in_w, L1_conv_conv_w, L1_conv_conv_b, L1_conv_dt_bias, L1_conv_A_log, L1_conv_Dp, L1_conv_rms_w, L1_conv_out_w, L1_conv_se1_w, L1_conv_se1_b, L1_conv_se2_w, L1_conv_se2_b)
    return x


_drawn_inputs = setup_inputs


def setup_inputs(seed=0):
    import zlib

    import numpy as np

    out = dict(_drawn_inputs(seed))
    spreads = {'L1_conv_norm_g': (1.0, 0.2),
     'L1_conv_norm_b': (0.0, 0.487),
     'L1_conv_conv_b': (0.0, 0.1),
     'L1_conv_Dp': (1.0, 0.6),
     'L1_conv_rms_w': (1.0, 0.2),
     'L1_conv_se1_b': (0.0, 0.8),
     'L1_conv_se2_b': (0.0, 0.8)}
    factors = {'L0_conv_bq': 29.698,
     'L0_conv_bk': 200.0,
     'L0_conv_bv': 43.051,
     'L1_conv_dt_bias': 64.0,
     'L1_conv_A_log': 64.0,
     'L1_conv_se1_w': 48.133,
     'L1_conv_se2_w': 8.0}
    for name, (base, spread) in spreads.items():
        noise = np.random.default_rng([zlib.crc32(name.encode()), seed]).standard_normal(out[name].shape)
        drawn = base * np.exp(spread * noise) if base else spread * noise
        out[name] = jnp.asarray(drawn.astype(out[name].dtype))
    for name, factor in factors.items():
        out[name] = (out[name] * factor).astype(out[name].dtype)
    return out
```

```python
from contextlib import ExitStack

import concourse.bass as bass
from concourse import mybir

ALU = mybir.AluOpType
ACT = mybir.ActivationFunctionType
AX = mybir.AxisListType
F32 = mybir.dt.float32
F16 = mybir.dt.float16
I32 = mybir.dt.int32

P = 128
B, C, N = 4, 256, 4096
CH = C // P
D = C // 8
BLK = 512
NB = N // BLK
QT = BLK // P
KT = N // P
KB = N // BLK
NST, HD, NH = 128, 64, 4
CONVD = C + 2 * NST
CM = CONVD // P
TAPS = 4
HALO = TAPS - 1
TH = QT * NH
RING = 4
P32S = 2
PSHIFT = 14 * 0.6931471805599453
MROW = 256.0
STK = 3 * D
VW = C + 2
EXPMASK = 0x7F800000
ONEBITS = 127 << 23

FILLS = ([("xT", 0)] * 2 + [("x1T", 0)] * 2 + [("uT", 0)] * 2 + [("dt", 1)] + [("xbc", 0)] * CM
         + [("z", 0)] * 2 + [("dAT", 1), ("cumT", 1)] + [("xsB", 0)] * QT
         + [("cb", 1), ("y", 1), ("st", 1)] * QT + [("yT", 0)] * 2 + [("out", 0)] * 2)
NF = len(FILLS)
FIRST = {}
for _n, (_name, _e) in enumerate(FILLS):
    FIRST.setdefault(_name, _n)
PER_EMPTIER = [sum(1 for _, e in FILLS if e == who) for who in (0, 1)]


def fill_of(name, k=0):
    return FIRST[name] + (3 * k if name in ("cb", "y", "st") else k)


def emptied_count(f):
    return sum(1 for _, e in FILLS[:f + 1] if e == FILLS[f][1])


def conv_attention_mamba_kernel(nc, x, wqkT, bqk, wvT, wv, gamma, inT, wqk, conv_w, conv_b,
                                dt_bias, A_log, Dp, outT, se1T, se1_b, se2T, columns, out):
    ctx = ExitStack()
    with ctx:
        def sb(name, shape, dt=F32):
            return ctx.enter_context(nc.sbuf_tensor(name, shape, dt))

        def ps(name):
            return ctx.enter_context(nc.psum_tensor(name, [P, 512], F32))

        def sem(name):
            return ctx.enter_context(nc.semaphore(name))

        x_sb = sb("x_sb", [P, CH, N])
        img = sb("img", [P, CH, N])
        v_hi = sb("v_hi", [P, KT, VW], F16)
        v_lo = sb("v_lo", [P, KT, VW], F16)
        qk_hi = sb("qk_hi", [2 * D, BLK], F16)
        qk_lo = sb("qk_lo", [2 * D, BLK], F16)
        kstack = sb("kstack", [STK + 2, N], F16)
        q_next = sb("q_next", [STK + 2, BLK], F16)
        q_cur = sb("q_cur", [STK + 2, BLK], F16)
        wqkT_sb = sb("wqkT_sb", [P, CH, 2 * D])
        wvT_sb = sb("wvT_sb", [P, CH, C])
        inT_sb = sb("inT_sb", [P, CH, 2 * C + 2 * NST + NH])
        outT_sb = sb("outT_sb", [P, CH, C])
        se1T_sb = sb("se1T_sb", [P, CH, C // 4])
        se2T_sb = sb("se2T_sb", [C // 4, C])
        cols = sb("cols", [P, 5, CH])
        gcol, bcol, rmscol, bvcol, s2col = (cols[:, k, :] for k in range(5))
        se1b = sb("se1b", [C // 4, 1])
        cw = sb("cw", [P, CM, TAPS])
        cb = sb("cb", [P, CM])
        bqk_sb = sb("bqk_sb", [2 * D, 1])
        gam = sb("gam", [P, 1])
        gbv = sb("gbv", [P, CH])
        dtb = sb("dtb", [P, NH])
        alog = sb("alog", [P, NH])
        arow = sb("arow", [P, NH])
        dcol = sb("dcol", [P, NH])
        ident = sb("ident", [P, P])
        identh = sb("identh", [P, P], F16)
        zrow = sb("zrow", [TH, P])
        wnat = img[:, 0, 0:4 * C]
        wmax = sb("wmax", [P, 5])
        wmaxa = sb("wmaxa", [P, 5])
        xmax = sb("xmax", [P, CH])
        xmaxa = sb("xmaxa", [P, CH])
        sc = sb("sc", [P, 8])
        sci = sb("sci", [P, 8], I32)
        qkscale = sb("qkscale", [2 * D, 1])
        xp = sb("xp", [P, 2, CH, BLK])
        qkf = sb("qkf", [2 * D, BLK])
        p32 = sb("p32", [P, P32S, BLK])
        p_hi = sb("p_hi", [P, RING, BLK], F16)
        p_lo = sb("p_lo", [P, RING, BLK], F16)
        maxes = sb("maxes", [P, QT, KB])
        mcol = sb("mcol", [P, 2, QT])
        mparts = sb("mparts", [P, QT, 2], F16)
        xb = xp[:, 0]
        shared = sb("shared", [P, 2, QT * C])
        xT = shared[:, 1, :].rearrange("p (t c) -> p t c", t=QT)
        uT = shared[:, 0, :].rearrange("p (h n) -> p h n", h=CH)
        yT = shared[:, 1, :].rearrange("p (h n) -> p h n", h=CH)
        dAb = shared[:, :, :].rearrange("p a n -> p (a n)")
        x1 = sb("x1", [P, QT, C])
        rden = sb("rden", [P, 2, QT])
        bst = sb("bst", [P, QT, 6])
        mv = sb("mv", [P, QT, 2])
        nw = sb("nw", [P, 4, QT])
        nwi = nw[:, :, :].bitcast(I32)
        xbc = sb("xbc", [P, CM, HALO + BLK])
        acc_c = sb("acc_c", [P, CM, BLK])
        th = xp[:, 1]
        zh = sb("zh", [P, QT, C])
        zt = sb("zt", [P, QT, C])
        dtt = sb("dtt", [P, 8, TH])
        dt16 = sb("dt16", [P, TH])
        dA16 = sb("dA16", [P, TH])
        cum16 = sb("cum16", [P, TH])
        dAr = sb("dAr", [TH, P])
        cumr = sb("cumr", [TH, P])
        totb = sb("totb", [P, TH])
        idt = sb("idt", [P, 2, NH, P])
        lt = sb("lt", [P, NH, P])
        mt = sb("mt", [P, NH, P])
        xsB = sb("xsB", [P, QT, C + NST])
        xd = sb("xd", [P, C])
        xw = sb("xw", [P, C])
        S = sb("S", [P, C])
        Sd = sb("Sd", [P, C])
        yt = sb("yt", [P, 2, C])
        y = sb("y", [P, QT, C])
        ms = sb("ms", [P, QT])
        pool1 = sb("pool1", [P, CH])
        pools = sb("pools", [P, CH])
        hdn = sb("hdn", [C // 4, 1])
        gate = sb("gate", [P, CH])
        u = y
        xc = acc_c

        acc = [ps(f"acc{t}") for t in range(QT)]
        p_et, p_mx = ps("p_et"), ps("p_mx")
        pl = [ps("pl0"), ps("pl1")]

        rows_d = nc.dram_tensor("rows_d", (TH * P,), F32, kind="Internal").ap()
        hi_d = nc.dram_tensor("hi_d", (2 * D, N), F16, kind="Internal").ap()
        lo_d = nc.dram_tensor("lo_d", (2 * D, N), F16, kind="Internal").ap()
        tot_d = nc.dram_tensor("tot_d", (TH,), F32, kind="Internal").ap()

        w_loaded = sem("w_loaded")
        ident_ready = sem("ident_ready")
        consts_ready = sem("consts_ready")
        wmax_ready = sem("wmax_ready")
        wmax_all = sem("wmax_all")
        prep_done = sem("prep_done")
        x_loaded = sem("x_loaded")
        xmax_ready = sem("xmax_ready")
        xmax_all = sem("xmax_all")
        scales_ready = sem("scales_ready")
        xp_ready = sem("xp_ready")
        qk_filled = sem("qk_filled")
        qk_emptied = sem("qk_emptied")
        v_filled = sem("v_filled")
        v_hi_done = sem("v_hi_done")
        v_lo_done = sem("v_lo_done")
        qk_stored = sem("qk_stored")
        k_loaded = sem("k_loaded")
        q_loaded = sem("q_loaded")
        mx_ready = sem("mx_ready")
        max_done = sem("max_done")
        m_ready = sem("m_ready")
        m_filled = sem("m_filled")
        q_next_done = sem("q_next_done")
        q_cur_ready = sem("q_cur_ready")
        et_ready = sem("et_ready")
        exp_done = sem("exp_done")
        hi_done = sem("hi_done")
        lo_done = sem("lo_done")
        pv_done = sem("pv_done")
        x1_done = sem("x1_done")
        xb_ready = sem("xb_ready")
        filled = sem("filled")
        act_emptied = sem("act_emptied")
        dve_emptied = sem("dve_emptied")
        u_ready = sem("u_ready")
        halo_done = sem("halo_done")
        tap0_done = sem("tap0_done")
        conv_done = sem("conv_done")
        tanh_done = sem("tanh_done")
        silu_done = sem("silu_done")
        zt_done = sem("zt_done")
        zs_done = sem("zs_done")
        dtabs_ready = sem("dtabs_ready")
        dtexp_done = sem("dtexp_done")
        dt_ready = sem("dt_ready")
        dA_done = sem("dA_done")
        rows_ready = sem("rows_ready")
        cum_ready = sem("cum_ready")
        rows_stored = sem("rows_stored")
        rows_loaded = sem("rows_loaded")
        idt_ready = sem("idt_ready")
        lt_ready = sem("lt_ready")
        mt_ready = sem("mt_ready")
        xd_ready = sem("xd_ready")
        xw_ready = sem("xw_ready")
        Sd_ready = sem("Sd_ready")
        S_ready = sem("S_ready")
        y1_ready = sem("y1_ready")
        y_ready = sem("y_ready")
        sq_done = sem("sq_done")
        yn_ready = sem("yn_ready")
        pool_done = sem("pool_done")
        state_zero = sem("state_zero")
        pooled_ready = sem("pooled_ready")
        se1_filled = sem("se1_filled")
        hdn_ready = sem("hdn_ready")
        se2_filled = sem("se2_filled")
        gate_th = sem("gate_th")
        gate_ready = sem("gate_ready")
        final_done = sem("final_done")
        out_stored = sem("out_stored")
        scan_done = sem("scan_done")
        settled = sem("settled")
        from_one = [ident_ready, consts_ready, wmax_ready, wmax_all, prep_done,
                    x_loaded, xmax_ready, xmax_all, scales_ready, xp_ready, qk_filled,
                    qk_emptied, v_filled, v_hi_done, v_lo_done, qk_stored, k_loaded,
                    q_loaded, mx_ready, max_done, m_ready, m_filled, q_next_done,
                    q_cur_ready, et_ready, exp_done, hi_done, lo_done, pv_done,
                    x1_done, xb_ready, filled, act_emptied, dve_emptied, u_ready,
                    halo_done, tap0_done, conv_done, tanh_done, silu_done, zt_done,
                    zs_done, dtabs_ready, dtexp_done, dt_ready, dA_done, rows_ready,
                    cum_ready, rows_stored, rows_loaded, idt_ready, lt_ready, mt_ready,
                    xd_ready, xw_ready, Sd_ready, S_ready, y1_ready, y_ready,
                    sq_done, yn_ready, pool_done, state_zero, pooled_ready, se1_filled,
                    hdn_ready, se2_filled, gate_th, gate_ready, final_done, out_stored,
                    scan_done, settled]

        xv = x.rearrange("b (h p) n -> b p h n", p=P)
        ov = out.rearrange("b (h p) n -> b p h n", p=P)
        block = ctx.enter_context(nc.Block())

        def n_emptied(g, f):
            return g * PER_EMPTIER[FILLS[f][1]] + emptied_count(f) + 1

        def n_filled(g, f):
            return g * NF + f + 2

        def bank(f):
            return pl[f % 2]

        def settle(e):
            e.sem_inc(settled, 1)

        @block.sync
        def _(e):
            def batch_start(b):
                e.wait_ge(final_done, b * CH * 2 + 1)
                settle(e)
                for h in range(CH):
                    e.dma_start(x_sb[:, h, :], xv[b, :, h, :]).then_inc(x_loaded, 16)
                with e.Fori(0, NB) as j:
                    e.wait_ge(qk_emptied, b * NB + j + 2)
                    settle(e)
                    for dst, src in ((hi_d, qk_hi), (lo_d, qk_lo)):
                        e.dma_start(dst[:, bass.ds(j * BLK, BLK)], src[:, :]).then_inc(qk_stored, 16)
                e.wait_ge(qk_stored, (b + 1) * NB * 32 + 1)
                e.wait_ge(et_ready, b * NB * KT + 1)
                settle(e)
                for src, row in ((hi_d, 0), (lo_d, D), (hi_d, 2 * D)):
                    e.dma_start(kstack[row:row + D, :], src[D:2 * D, :]).then_inc(k_loaded, 16)

            def load_q(g, i):
                e.wait_ge(q_cur_ready, g + 1)
                settle(e)
                for src, row in ((hi_d, 0), (hi_d, D), (lo_d, 2 * D)):
                    e.dma_start(q_next[row:row + D, :], src[0:D, bass.ds(i * BLK, BLK)])\
                        .then_inc(q_loaded, 16)

            def decay_rows(g):
                e.wait_ge(rows_ready, g + 2)
                e.dma_start(rows_d.rearrange("(r i) -> r i", i=P), dAr[:, :]).then_inc(rows_stored, 16)
                e.wait_ge(cum_ready, g + 2)
                e.dma_start(tot_d.rearrange("(r a) -> r a", a=1), cumr[:, P - 1:P]).then_inc(rows_stored, 16)
                e.wait_ge(rows_stored, (g + 1) * 32 + 1)
                e.wait_ge(filled, g * NF + fill_of("z", 1) + 2)
                settle(e)
                e.wait_ge(scan_done, g * QT + 1)
                e.wait_ge(Sd_ready, g * QT + 1)
                e.dma_start(dAb, rows_d.partition_broadcast(P)).then_inc(rows_loaded, 16)
                e.dma_start(totb[:, :], tot_d.partition_broadcast(P)).then_inc(rows_loaded, 16)

            with e.Fori(0, B) as b:
                batch_start(b)
                load_q(b * NB, 0)
                with e.Fori(0, NB - 1) as i:
                    load_q(b * NB + i + 1, i + 1)
                    decay_rows(b * NB + i)
                decay_rows(b * NB + NB - 1)
                for n in range(CH * 2):
                    h, half = n // 2, n % 2
                    e.wait_ge(final_done, b * CH * 2 + n + 2)
                    settle(e)
                    e.dma_start(ov[b, :, h, half * (N // 2):(half + 1) * (N // 2)],
                                img[:, h, half * (N // 2):(half + 1) * (N // 2)]).then_inc(out_stored, 16)
            e.wait_ge(out_stored, B * CH * 2 * 16 + 1)

        @block.gpsimd
        def _(e):
            for semaphore in from_one:
                e.sem_inc(semaphore, 1)
            e.memset(ident[:, :], 0.0)
            e.memset(identh[:, :], 0.0)
            e.memset(v_hi[:, :, :], 1.0)
            e.memset(v_lo[:, :, :], 0.0)
            e.drain()
            e.memset(kstack[STK:STK + 2, :], -MROW)
            e.drain()
            e.memset(wnat, 0.0)
            e.memset(wmax[:, :], 0.0)
            e.drain()
            for m in (ident, identh):
                e.affine_select(out=m[:, :], in_=m[:, :], compare_op=ALU.not_equal, fill=1.0, base=0,
                                pattern=[[-1, P]], channel_multiplier=1)
            e.drain().then_inc(ident_ready, 1)
            wdmas = [(wqkT_sb[:, :, :], wqkT.rearrange("(h p) n -> p h n", p=P)),
                     (wvT_sb[:, :, :], wvT.rearrange("(h p) n -> p h n", p=P)),
                     (inT_sb[:, :, :], inT.rearrange("(h p) n -> p h n", p=P)),
                     (outT_sb[:, :, :], outT.rearrange("(h p) n -> p h n", p=P)),
                     (se1T_sb[:, :, :], se1T.rearrange("(h p) n -> p h n", p=P)),
                     (se2T_sb[:, :], se2T),
                     (cw[:, :, :], conv_w.rearrange("(m p) k -> p m k", p=P)),
                     (cb[:, :], conv_b),
                     (bqk_sb[:, :], bqk.rearrange("(p a) -> p a", a=1)),
                     (se1b[:, :], se1_b.rearrange("(p a) -> p a", a=1)),
                     (gam[:, :], gamma.partition_broadcast(P)),
                     (dtb[:, :], dt_bias.partition_broadcast(P)),
                     (alog[:, :], A_log.partition_broadcast(P)),
                     (dcol[:, :], Dp.partition_broadcast(P)),
                     (wnat[:, 0:2 * C].rearrange("p (h n) -> p h n", h=2), wv.rearrange("(h p) n -> p h n", p=P)),
                     (wnat[0:D, 2 * C:3 * C], wqk[0:D, :]),
                     (wnat[0:D, 3 * C:4 * C], wqk[D:2 * D, :]),
                     (wmax[0:D, 3:4], bqk[0:D].rearrange("(p a) -> p a", a=1)),
                     (wmax[0:D, 4:5], bqk[D:2 * D].rearrange("(p a) -> p a", a=1))]
            wdmas.append((cols[:, :, :], columns))
            for dst, src in wdmas:
                e.dma_start(dst, src).then_inc(w_loaded, 16)
            e.wait_ge(w_loaded, 16 * len(wdmas))
            e.drain().then_inc(consts_ready, 1)
            e.wait_ge(wmax_ready, 2)
            e.partition_all_reduce(wmaxa[:, :], wmax[:, :], P, bass.bass_isa.ReduceOp.absmax).then_inc(wmax_all, 1)

            def batch_start(b):
                e.wait_ge(xmax_ready, b + 2)
                settle(e)
                e.partition_all_reduce(xmaxa[:, :], xmax[:, :], P, bass.bass_isa.ReduceOp.max).then_inc(xmax_all, 1)
                e.wait_ge(filled, b * NB * NF + 1)
                settle(e)
                e.memset(S[:, :], 0.0).then_inc(state_zero, 1)
                with e.Fori(0, NB // 2) as jj:
                    for r in range(2):
                        j = jj * 2 + r
                        e.wait_ge(x_loaded, (b + 1) * CH * 16 + 1)
                        e.wait_ge(v_filled, b * NB * 2 + j * 2 - (2 if r else 0) + 1)
                        settle(e)
                        e.tensor_copy(xp[:, r, :, :], x_sb[:, :, bass.ds(j * BLK, BLK)]).then_inc(xp_ready, 1)

            def layer1(g):
                for m in range(CM):
                    e.wait_ge(act_emptied, n_emptied(g, fill_of("xbc", m)))
                    e.wait_ge(filled, g * NF + 1)
                    settle(e)
                    e.tensor_scalar(acc_c[:, m, :], xbc[:, m, HALO:HALO + BLK], cw[:, m, HALO:TAPS], cb[:, m:m + 1],
                                    ALU.mult, ALU.add).then_inc(tap0_done, 1)
                e.wait_ge(dt_ready, g + 2)
                for c in range(QT):
                    r = c % 2
                    e.wait_ge(scan_done, g * QT + max(c - 1, 0) + 1)
                    e.tensor_tensor(idt[:, r], ident[:, :].unsqueeze(1).to_broadcast([P, NH, P]),
                                    dt16[:, c * NH:(c + 1) * NH].unsqueeze(2).to_broadcast([P, NH, P]),
                                    ALU.mult).then_inc(idt_ready, 1)
                    xs = xsB[:, c, 0:C].rearrange("p (h d) -> p h d", h=NH)
                    e.wait_ge(act_emptied, n_emptied(g, fill_of("xsB", c)))
                    e.wait_ge(y1_ready, g * QT + c + 1)
                    e.tensor_tensor(xd[:, :].rearrange("p (h d) -> p h d", h=NH), xs,
                                    dcol[:, :].unsqueeze(2).to_broadcast([P, NH, HD]), ALU.mult).then_inc(xd_ready, 1)
                    e.wait_ge(lt_ready, g * QT + c + 2)
                    e.wait_ge(S_ready, g * QT + c + 1)
                    e.tensor_tensor(xw[:, :].rearrange("p (h d) -> p h d", h=NH), xs,
                                    lt[:, :, P - 1:P].to_broadcast([P, NH, HD]), ALU.mult).then_inc(xw_ready, 1)
                    e.wait_ge(rows_loaded, (g + 1) * 32 + 1)
                    e.tensor_tensor(Sd[:, :].rearrange("p (h d) -> p h d", h=NH),
                                    S[:, :].rearrange("p (h d) -> p h d", h=NH),
                                    totb[:, c * NH:(c + 1) * NH].unsqueeze(2).to_broadcast([P, NH, HD]),
                                    ALU.mult).then_inc(Sd_ready, 1)
                    e.wait_ge(y1_ready, g * QT + c + 2)
                    e.wait_ge(zs_done, g + 2)
                    e.tensor_tensor(yt[:, 0, :], yt[:, 0, :], yt[:, 1, :], ALU.add)
                    e.drain()
                    e.tensor_tensor(y[:, c, :], yt[:, 0, :], zt[:, c, :], ALU.mult).then_inc(y_ready, 1)

            with e.Fori(0, B) as b:
                batch_start(b)
                with e.Fori(0, NB) as i:
                    layer1(b * NB + i)

        @block.scalar
        def _(e):
            e.wait_ge(wmax_ready, 2)
            e.activation(arow[:, :], alog[:, :], ACT.Exp).then_inc(prep_done, 1)

            def batch_start(b):
                e.wait_ge(scales_ready, b + 2)
                e.wait_ge(pv_done, b * NB * KT + RING + 1)
                settle(e)
                with e.Fori(0, NB) as j:
                    for t in range(2):
                        e.wait_ge(v_filled, b * NB * 2 + j * 2 + t + 2)
                        settle(e)
                        e.activation(v_hi[:, bass.ds(j * 4 + t * 2, 2), 0:C],
                                     pl[t][:, :].rearrange("p (n c) -> p n c", n=2), ACT.Copy,
                                     scale=sc[:, 0:1]).then_inc(v_hi_done, 1)

            def exp_tile(g, k):
                e.wait_ge(et_ready, g * KT + k + 2)
                e.wait_ge(lo_done, g * KT + k + 2)
                e.activation(p32[:, k % P32S, :], p_et[:, :], ACT.Exp).then_inc(exp_done, 1)

            def hi_tile(g, k):
                e.wait_ge(exp_done, g * KT + k + 2)
                e.wait_ge(pv_done, g * KT + k + 2)
                e.activation(p_hi[:, k % RING, :], p32[:, k % P32S, :], ACT.Copy).then_inc(hi_done, 1)

            def attention(g):
                for k in range(KT):
                    exp_tile(g, k)
                    if k >= 1:
                        hi_tile(g, k - 1)
                hi_tile(g, KT - 1)

            def layer1(g, i):
                e.wait_ge(filled, g * NF + 1)
                settle(e)
                for h in range(CH):
                    e.activation(xb[:, h, :], x_sb[:, h, bass.ds(i * BLK, BLK)], ACT.Identity,
                                 bias=gbv[:, h:h + 1]).then_inc(xb_ready, 1)
                for k in range(2):
                    f = fill_of("xT", k)
                    e.wait_ge(filled, n_filled(g, f))
                    e.wait_ge(x1_done, g + 1)
                    e.activation(xT[:, 2 * k:2 * k + 2, :], bank(f)[:, :].rearrange("p (t c) -> p t c", t=2),
                                 ACT.Copy).then_inc(act_emptied, 1)
                for h in range(CH):
                    f = fill_of("x1T", h)
                    e.wait_ge(filled, n_filled(g, f))
                    settle(e)
                    e.activation(x_sb[:, h, bass.ds(i * BLK, BLK)], bank(f)[:, :], ACT.Copy).then_inc(act_emptied, 1)
                for h in range(CH):
                    f = fill_of("uT", h)
                    e.wait_ge(filled, n_filled(g, f))
                    e.activation(uT[:, h, :], bank(f)[:, :], ACT.Identity, bias=bcol[:, h:h + 1],
                                 scale=gcol[:, h:h + 1]).then_inc(act_emptied, 1)
                e.wait_ge(dtabs_ready, g + 2)
                e.activation(dtt[:, 2, :], dtt[:, 1, :], ACT.Exp, scale=-1.0).then_inc(dtexp_done, 1)
                for m in range(CM):
                    f = fill_of("xbc", m)
                    e.wait_ge(filled, n_filled(g, f))
                    if m == 0:
                        e.wait_ge(halo_done, halo_count(g) + 1)
                    e.activation(xbc[:, m, HALO:HALO + BLK], bank(f)[:, :], ACT.Copy).then_inc(act_emptied, 1)
                for k in range(2):
                    f = fill_of("z", k)
                    e.wait_ge(filled, n_filled(g, f))
                    e.wait_ge(y_ready, g * QT + 1)
                    e.activation(zh[:, 2 * k:2 * k + 2, :], bank(f)[:, :].rearrange("p (t c) -> p t c", t=2),
                                 ACT.Copy, scale=0.5).then_inc(act_emptied, 1)
                e.wait_ge(dt_ready, g + 2)
                e.activation(dA16[:, :], dtt[:, 7, :], ACT.Exp).then_inc(dA_done, 1)
                e.wait_ge(act_emptied, n_emptied(g, fill_of("z", 1)))
                e.activation(zt[:, :, :], zh[:, :, :], ACT.Tanh).then_inc(zt_done, 1)
                for m in range(CM):
                    e.wait_ge(conv_done, g * CM + m + 2)
                    e.wait_ge(silu_done, g * CM + max(m - 1, 0) + 1)
                    e.activation(th[:, m % 2, :], acc_c[:, m, :], ACT.Tanh).then_inc(tanh_done, 1)
                for c in range(QT):
                    f = fill_of("xsB", c)
                    e.wait_ge(filled, n_filled(g, f))
                    e.activation(xsB[:, c, :], bank(f)[:, 0:C + NST], ACT.Copy).then_inc(act_emptied, 1)
                for c in range(QT):
                    e.wait_ge(y_ready, g * QT + c + 2)
                    e.activation(x1[:, c, :], y[:, c, :], ACT.Square, accum_out=ms[:, c:c + 1]).then_inc(sq_done, 1)
                for h in range(CH):
                    f = fill_of("yT", h)
                    e.wait_ge(filled, n_filled(g, f))
                    e.activation(yT[:, h, :], bank(f)[:, :], ACT.Copy, scale=rmscol[:, h:h + 1])\
                        .then_inc(act_emptied, 1)
                for h in range(CH):
                    f = fill_of("out", h)
                    e.wait_ge(filled, n_filled(g, f))
                    e.wait_ge(pool_done, g + 1)
                    e.wait_ge(out_stored, stored_count(g) + 1)
                    settle(e)
                    e.activation(img[:, h, bass.ds(i * BLK, BLK)], bank(f)[:, :], ACT.Copy,
                                 accum_out=pool1[:, h:h + 1]).then_inc(act_emptied, 1)

            with e.Fori(0, B) as b:
                batch_start(b)

                def halo_count(g):
                    return g + b + 1

                def stored_count(g):
                    return b * CH * 2 * 16

                with e.Fori(0, NB) as i:
                    attention(b * NB + i)
                    layer1(b * NB + i, i)
                e.wait_ge(se1_filled, b + 2)
                e.activation(hdn[:, :], pl[0][0:C // 4, 0:1], ACT.Relu, bias=se1b[:, :]).then_inc(hdn_ready, 1)
                e.wait_ge(se2_filled, b + 2)
                for h in range(CH):
                    e.activation(gate[:, h:h + 1], pl[1][:, h:h + 1], ACT.Identity, bias=s2col[:, h:h + 1])
                e.drain()
                e.activation(gate[:, :], gate[:, :], ACT.Tanh, scale=0.5).then_inc(gate_th, 1)

        @block.tensor
        def _(e):
            e.wait_ge(ident_ready, 2)
            e.wait_ge(consts_ready, 2)
            e.sem_inc(pv_done, RING)

            def projections(b):
                e.wait_ge(exp_done, b * NB * KT + 1)
                e.wait_ge(act_emptied, b * NB * PER_EMPTIER[0] + 1)
                e.wait_ge(gate_th, b + 1)
                settle(e)
                with e.Fori(0, NB // 2) as jj:
                    for r in range(2):
                        j = jj * 2 + r
                        e.wait_ge(xp_ready, b * NB + j + 2)
                        e.wait_ge(qk_emptied, b * NB + j + 1)
                        for h in range(CH):
                            mm = e.matmul(p_et[0:2 * D, :], wqkT_sb[:, h, :], xp[:, r, h, :],
                                          start=(h == 0), stop=(h == CH - 1))
                        mm.then_inc(qk_filled, 1)
                        for t in range(2):
                            e.wait_ge(v_lo_done, b * NB * 2 + j * 2 + t - (1 if t else 0) + 1)
                            for k in range(2):
                                tok = (2 * t + k) * P
                                for h in range(CH):
                                    mm = e.matmul(pl[t][:, k * C:(k + 1) * C], xp[:, r, h, tok:tok + P],
                                                  wvT_sb[:, h, :], start=(h == 0), stop=(h == CH - 1))
                            mm.then_inc(v_filled, 1)

            def max_tile(g, n):
                e.wait_ge(max_done, g * KT + n + 1)
                if n == 0:
                    e.wait_ge(q_loaded, (g + 1) * 48 + 1)
                    e.wait_ge(q_next_done, g + 1)
                q, kb = n // KB, n % KB
                e.matmul(p_mx[:, :], q_next[0:STK, q * P:(q + 1) * P], kstack[0:STK, kb * BLK:(kb + 1) * BLK],
                         start=True, stop=True).then_inc(mx_ready, 1)

            def max_rows(g):
                e.wait_ge(m_ready, g + 2)
                for t in range(QT):
                    mm = e.matmul(p_mx[STK:STK + 2, t * P:(t + 1) * P], mparts[:, t, :], identh[:, :],
                                  start=True, stop=True)
                mm.then_inc(m_filled, 1)

            def energies(g, k):
                e.wait_ge(exp_done, g * KT + k + 1)
                e.matmul(p_et[:, :], kstack[:, k * P:(k + 1) * P], q_cur[:, :],
                         start=True, stop=True).then_inc(et_ready, 1)

            def values(g, k):
                e.wait_ge(hi_done, g * KT + k + 2)
                if k == 0:
                    e.wait_ge(x1_done, g + 1)
                r = k % RING
                for t in range(QT):
                    e.matmul(acc[t][:, 0:C + 1], p_hi[:, r, t * P:(t + 1) * P], v_hi[:, k, 0:C + 1],
                             start=(k == 0), stop=False)
                    e.matmul(acc[t][:, 0:C], p_hi[:, r, t * P:(t + 1) * P], v_lo[:, k, 0:C],
                             start=False, stop=False, skip_group_check=True)
                e.wait_ge(lo_done, g * KT + k + 1 + P32S + 1)
                for t in range(QT):
                    mm = e.matmul(acc[t][:, 0:C + 1], p_lo[:, r, t * P:(t + 1) * P], v_hi[:, k, 0:C + 1],
                                  start=False, stop=(k == KT - 1))
                mm.then_inc(pv_done, 1)

            def attention(g, more):
                e.wait_ge(q_cur_ready, g + 2)
                energies(g, 0)
                energies(g, 1)
                for k in range(KT):
                    if k + 2 < KT:
                        energies(g, k + 2)
                    if more:
                        max_tile(g + 1, k)
                    values(g, k)
                if more:
                    max_rows(g + 1)

            def begin(g, f):
                if f >= 2:
                    e.wait_ge(dve_emptied if FILLS[f - 2][1] else act_emptied, n_emptied(g, f - 2))
                else:
                    e.wait_ge(act_emptied, g * PER_EMPTIER[0] + 1)
                return bank(f)

            def layer1(g):
                for k in range(2):
                    f = fill_of("xT", k)
                    o = begin(g, f)
                    e.wait_ge(xb_ready, (g + 1) * CH + 1)
                    for t in range(2):
                        for h in range(CH):
                            mm = e.transpose(o[:, t * C + h * P:t * C + (h + 1) * P],
                                             xb[:, h, (2 * k + t) * P:(2 * k + t + 1) * P], ident[:, :])
                    mm.then_inc(filled, 1)
                for name, src, ready in (("x1T", x1, x1_done), ("uT", u, u_ready)):
                    for h in range(CH):
                        f = fill_of(name, h)
                        o = begin(g, f)
                        e.wait_ge(ready, g + 2)
                        for t in range(QT):
                            mm = e.transpose(o[:, t * P:(t + 1) * P], src[:, t, h * P:(h + 1) * P], ident[:, :])
                        mm.then_inc(filled, 1)
                e.wait_ge(act_emptied, n_emptied(g, fill_of("uT", 1)))
                f = fill_of("dt")
                o = begin(g, f)
                for t in range(QT):
                    for h in range(CH):
                        mm = e.matmul(o[:, t * NH:(t + 1) * NH], uT[:, h, t * P:(t + 1) * P],
                                      inT_sb[:, h, C + CONVD:C + CONVD + NH], start=(h == 0), stop=(h == CH - 1))
                mm.then_inc(filled, 1)
                for m in range(CM):
                    f = fill_of("xbc", m)
                    o = begin(g, f)
                    for h in range(CH):
                        mm = e.matmul(o[:, :], inT_sb[:, h, C + m * P:C + (m + 1) * P], uT[:, h, :],
                                      start=(h == 0), stop=(h == CH - 1))
                    mm.then_inc(filled, 1)
                for k in range(2):
                    f = fill_of("z", k)
                    o = begin(g, f)
                    for t in range(2):
                        for h in range(CH):
                            mm = e.matmul(o[:, t * C:(t + 1) * C], uT[:, h, (2 * k + t) * P:(2 * k + t + 1) * P],
                                          inT_sb[:, h, 0:C], start=(h == 0), stop=(h == CH - 1))
                    mm.then_inc(filled, 1)
                f = fill_of("dAT")
                o = begin(g, f)
                e.wait_ge(dA_done, g + 2)
                e.transpose(o[0:TH, 0:P], dA16[:, :], ident[:, :]).then_inc(filled, 1)
                f = fill_of("cumT")
                o = begin(g, f)
                e.wait_ge(cum_ready, g + 2)
                settle(e)
                e.transpose(o[:, 0:TH], cumr[:, :], ident[0:TH, 0:TH]).then_inc(filled, 1)
                e.wait_ge(silu_done, (g + 1) * CM + 1)
                for c in range(QT):
                    f = fill_of("xsB", c)
                    o = begin(g, f)
                    for m in range(CM - 1):
                        mm = e.transpose(o[:, m * P:(m + 1) * P], xc[:, m, c * P:(c + 1) * P], ident[:, :])
                    mm.then_inc(filled, 1)
                for c in range(QT):
                    f = fill_of("cb", c)
                    o = begin(g, f)
                    e.matmul(o[:, 0:P], xc[:, 2, c * P:(c + 1) * P], xc[:, 3, c * P:(c + 1) * P],
                             start=True, stop=True).then_inc(filled, 1)
                    f = fill_of("y", c)
                    o = begin(g, f)
                    e.wait_ge(act_emptied, n_emptied(g, fill_of("xsB", c)))
                    if c == 0:
                        e.wait_ge(state_zero, zero_count(g) + 1)
                    else:
                        e.wait_ge(S_ready, g * QT + c + 1)
                    e.matmul(o[:, C:2 * C], xc[:, 3, c * P:(c + 1) * P], S[:, :], start=True, stop=True)
                    e.wait_ge(mt_ready, g * QT + c + 2)
                    for h in range(NH):
                        mm = e.matmul(o[:, h * HD:(h + 1) * HD], mt[:, h, :], xsB[:, c, h * HD:(h + 1) * HD],
                                      start=True, stop=True)
                    mm.then_inc(filled, 1)
                    f = fill_of("st", c)
                    o = begin(g, f)
                    e.wait_ge(xw_ready, g * QT + c + 2)
                    e.matmul(o[:, 0:C], xsB[:, c, C:C + NST], xw[:, :], start=True, stop=True).then_inc(filled, 1)
                e.wait_ge(yn_ready, g + 2)
                for h in range(CH):
                    f = fill_of("yT", h)
                    o = begin(g, f)
                    for t in range(QT):
                        mm = e.transpose(o[:, t * P:(t + 1) * P], x1[:, t, h * P:(h + 1) * P], ident[:, :])
                    mm.then_inc(filled, 1)
                e.wait_ge(act_emptied, n_emptied(g, fill_of("yT", 1)))
                for m in range(CH):
                    f = fill_of("out", m)
                    o = begin(g, f)
                    for h in range(CH):
                        mm = e.matmul(o[:, :], outT_sb[:, h, m * P:(m + 1) * P], yT[:, h, :],
                                      start=(h == 0), stop=(h == CH - 1))
                    mm.then_inc(filled, 1)

            with e.Fori(0, B) as b:
                projections(b)
                e.wait_ge(k_loaded, (b + 1) * 48 + 1)
                for n in range(KT):
                    max_tile(b * NB, n)
                max_rows(b * NB)

                def zero_count(g):
                    return b + 1

                with e.Fori(0, NB - 1) as i:
                    attention(b * NB + i, True)
                    e.wait_ge(S_ready, (b * NB + i) * QT + 1)
                    layer1(b * NB + i)
                attention(b * NB + NB - 1, False)
                e.wait_ge(S_ready, (b * NB + NB - 1) * QT + 1)
                layer1(b * NB + NB - 1)
                e.wait_ge(pooled_ready, b + 2)
                e.wait_ge(act_emptied, (b + 1) * NB * PER_EMPTIER[0] + 1)
                for h in range(CH):
                    mm = e.matmul(pl[0][0:C // 4, 0:1], se1T_sb[:, h, :], pools[:, h:h + 1],
                                  start=(h == 0), stop=(h == CH - 1))
                mm.then_inc(se1_filled, 1)
                e.wait_ge(hdn_ready, b + 2)
                for h in range(CH):
                    mm = e.matmul(pl[1][:, h:h + 1], se2T_sb[:, h * P:(h + 1) * P], hdn[:, :],
                                  start=True, stop=True)
                mm.then_inc(se2_filled, 1)

        @block.vector
        def _(e):
            v = nc.vector
            e.wait_ge(consts_ready, 2)
            v.tensor_reduce(wmax[:, 0:1], wnat[:, 0:2 * C], AX.X, ALU.max, apply_absolute_value=True)
            v.tensor_reduce(wmax[:, 1:2], wnat[:, 2 * C:3 * C], AX.X, ALU.max, apply_absolute_value=True)
            v.tensor_reduce(wmax[:, 2:3], wnat[:, 3 * C:4 * C], AX.X, ALU.max, apply_absolute_value=True)
            v.tensor_scalar(alog[:, :], alog[:, :], 80.0, None, ALU.min)
            v.tensor_scalar(gbv[:, :], bvcol, gam[:, 0:1], None, ALU.mult)
            v.tensor_scalar(cw[:, :, :], cw[:, :, :], 0.5, None, ALU.mult)
            v.tensor_scalar(cb[:, :], cb[:, :], 0.5, None, ALU.mult)
            e.drain().then_inc(wmax_ready, 1)
            e.wait_ge(prep_done, 2)
            v.tensor_scalar(arow[:, :], arow[:, :], -1.0, None, ALU.mult)
            e.wait_ge(wmax_all, 2)
            e.drain()
            e.sem_inc(lo_done, P32S)

            def scales(b):
                for h in range(CH):
                    e.wait_ge(x_loaded, (b + 1) * CH * 16 + 1)
                    v.tensor_reduce(xmax[:, h:h + 1], x_sb[:, h, :], AX.X, ALU.max, apply_absolute_value=True)
                e.drain().then_inc(xmax_ready, 1)
                e.wait_ge(xmax_all, b + 2)
                v.tensor_reduce(sc[:, 1:2], xmaxa[:, :], AX.X, ALU.max)
                e.drain()
                v.tensor_scalar(sc[:, 1:2], sc[:, 1:2], float(C), None, ALU.mult)
                e.drain()
                v.tensor_scalar(sc[:, 2:5], wmaxa[:, 0:3], sc[:, 1:2], 1e-30, ALU.mult, ALU.max)
                e.drain()
                v.tensor_tensor(sc[:, 3:5], sc[:, 3:5], wmaxa[:, 3:5], ALU.add)
                e.drain()
                v.tensor_scalar(sci[:, 2:5], sc[:, 2:5].bitcast(I32), EXPMASK, None, ALU.bitwise_and)
                e.drain()
                v.tensor_scalar(sc[:, 0:1].bitcast(I32), sci[:, 2:3], -1.0, float((2 * 127 + 14) << 23),
                                ALU.mult, ALU.add)
                v.tensor_tensor(sci[:, 5:6], sci[:, 4:5], sci[:, 3:4], ALU.subtract)
                e.drain()
                v.tensor_scalar(sci[:, 6:7], sci[:, 5:6], 0.5, float(ONEBITS), ALU.mult, ALU.add)
                e.drain()
                v.tensor_scalar(sci[:, 7:8], sci[:, 6:7], EXPMASK, None, ALU.bitwise_and)
                e.drain()
                v.tensor_copy(qkscale[0:D, :].bitcast(I32), sci[0:D, 7:8])
                v.tensor_scalar(qkscale[D:2 * D, :].bitcast(I32), sci[D:2 * D, 7:8], -1.0, float(2 * ONEBITS),
                                ALU.mult, ALU.add)
                v.reciprocal(sc[:, 6:7], sc[:, 0:1])
                e.drain()
                v.tensor_tensor(sc[:, 7:8], sc[:, 6:7], gam[:, :], ALU.mult)
                e.drain().then_inc(scales_ready, 1)

            def split_projections(b):
                e.wait_ge(k_loaded, b * 48 + 1)
                e.wait_ge(q_loaded, b * NB * 48 + 1)
                e.wait_ge(pv_done, b * NB * KT + RING + 1)
                settle(e)
                with e.Fori(0, NB) as j:
                    e.wait_ge(qk_filled, b * NB + j + 2)
                    v.tensor_scalar(qkf[:, :], p_et[0:2 * D, :], bqk_sb[:, :], qkscale[:, :], ALU.add, ALU.mult)
                    e.drain()
                    e.wait_ge(qk_stored, b * NB * 32 + j * 32 + 1)
                    v.tensor_copy(qk_hi[:, :], qkf[:, :])
                    e.drain()
                    v.tensor_tensor(qk_lo[:, :], qkf[:, :], qk_hi[:, :],
                                    ALU.subtract).then_inc(qk_emptied, 1)
                    for t in range(2):
                        e.wait_ge(v_hi_done, b * NB * 2 + j * 2 + t + 2)
                        settle(e)
                        v.scalar_tensor_tensor(v_lo[:, bass.ds(j * 4 + t * 2, 2), 0:C],
                                               pl[t][:, :].rearrange("p (n c) -> p n c", n=2), sc[:, 0:1],
                                               v_hi[:, bass.ds(j * 4 + t * 2, 2), 0:C],
                                               ALU.mult, ALU.subtract).then_inc(v_lo_done, 1)

            def max_tile(g, n):
                e.wait_ge(mx_ready, g * KT + n + 2)
                v.tensor_reduce(maxes[:, n // KB, n % KB:n % KB + 1], p_mx[:, :], AX.X, ALU.max)\
                    .then_inc(max_done, 1)

            def max_finish(g):
                e.drain()
                v.tensor_reduce(mcol[:, 0, :], maxes[:, :, :], AX.X, ALU.max)
                e.drain()
                v.tensor_scalar(mcol[:, 1, :], mcol[:, 0, :], -PSHIFT, 1.0 / MROW, ALU.add, ALU.mult)
                e.drain()
                v.tensor_copy(mparts[:, :, 0], mcol[:, 1, :])
                e.drain()
                v.tensor_tensor(mparts[:, :, 1], mcol[:, 1, :], mparts[:, :, 0], ALU.subtract)\
                    .then_inc(m_ready, 1)
                e.wait_ge(m_filled, g + 2)
                v.tensor_copy(q_next[STK:STK + 2, :], p_mx[STK:STK + 2, :]).then_inc(q_next_done, 1)

            def lo_tile(g, k):
                e.wait_ge(hi_done, g * KT + k + 2)
                e.wait_ge(pv_done, g * KT + k + 2)
                v.tensor_tensor(p_lo[:, k % RING, :], p32[:, k % P32S, :], p_hi[:, k % RING, :],
                                ALU.subtract).then_inc(lo_done, 1)

            def attention(g, more):
                e.wait_ge(et_ready, g * KT + 1)
                e.wait_ge(q_next_done, g + 2)
                v.tensor_copy(q_cur[:, :], q_next[:, :]).then_inc(q_cur_ready, 1)
                for k in range(KT):
                    if more:
                        max_tile(g + 1, k)
                    lo_tile(g, k)
                if more:
                    max_finish(g + 1)

            def rsqrt(src, scale, eps):
                v.tensor_scalar(nw[:, 0, :], src, scale, eps, ALU.mult, ALU.add)
                e.drain()
                v.tensor_scalar(nwi[:, 1, :], nwi[:, 0, :], 1, None, ALU.logical_shift_right)
                v.tensor_scalar(nw[:, 2, :], nw[:, 0, :], -0.5, None, ALU.mult)
                e.drain()
                v.tensor_scalar(nwi[:, 3, :], nwi[:, 1, :], -1.0, float(0x5F3759DF), ALU.mult, ALU.add)
                for _ in range(4):
                    e.drain()
                    v.tensor_tensor(nw[:, 0, :], nw[:, 3, :], nw[:, 3, :], ALU.mult)
                    e.drain()
                    v.tensor_tensor(nw[:, 1, :], nw[:, 0, :], nw[:, 2, :], ALU.mult)
                    e.drain()
                    v.scalar_tensor_tensor(nw[:, 3, :], nw[:, 1, :], 1.5, nw[:, 3, :], ALU.add, ALU.mult)
                e.drain()

            def layer1(g):
                e.wait_ge(pv_done, (g + 1) * KT + RING + 1)
                e.wait_ge(act_emptied, n_emptied(g, fill_of("xT", 1)))
                for t in range(QT):
                    v.reciprocal(rden[:, 0, t:t + 1], acc[t][:, C:C + 1])
                e.drain()
                v.tensor_scalar(rden[:, 1, :], rden[:, 0, :], sc[:, 7:8], None, ALU.mult)
                e.drain()
                for t in range(QT):
                    ins = v.scalar_tensor_tensor(x1[:, t, :], acc[t][:, 0:C], rden[:, 1, t:t + 1], xT[:, t, :],
                                                 ALU.mult, ALU.add)
                ins.then_inc(x1_done, 1)
                e.drain()
                for t in range(QT):
                    v.bn_stats(bst[:, t, :], x1[:, t, :])
                e.drain()
                for t in range(QT):
                    v.bn_aggr(mv[:, t, :], bst[:, t, :])
                e.drain()
                rsqrt(mv[:, :, 1], 1.0, 1e-5)
                for t in range(QT):
                    ins = v.tensor_scalar(u[:, t, :], x1[:, t, :], mv[:, t, 0:1], nw[:, 3, t:t + 1],
                                          ALU.subtract, ALU.mult)
                ins.then_inc(u_ready, 1)
                f = fill_of("dt")
                e.wait_ge(filled, n_filled(g, f))
                v.tensor_tensor(dtt[:, 0, :].rearrange("p (t h) -> p t h", h=NH),
                                bank(f)[:, 0:TH].rearrange("p (t h) -> p t h", h=NH),
                                dtb[:, :].unsqueeze(1).to_broadcast([P, QT, NH]), ALU.add).then_inc(dve_emptied, 1)
                e.drain()
                v.scalar_tensor_tensor(dtt[:, 1, :], dtt[:, 0, :], -1.0, dtt[:, 0, :], ALU.mult, ALU.max)\
                    .then_inc(dtabs_ready, 1)
                v.tensor_scalar(dtt[:, 3, :], dtt[:, 0, :], 0.0, None, ALU.max)
                e.wait_ge(dtexp_done, g + 2)
                v.tensor_scalar(dtt[:, 4, :], dtt[:, 2, :], 2.0, None, ALU.add)
                e.drain()
                v.reciprocal(dtt[:, 5, :], dtt[:, 4, :])
                e.drain()
                v.tensor_tensor(dtt[:, 4, :], dtt[:, 2, :], dtt[:, 5, :], ALU.mult)
                e.drain()
                v.tensor_tensor(dtt[:, 5, :], dtt[:, 4, :], dtt[:, 4, :], ALU.mult)
                e.drain()
                v.tensor_scalar(dtt[:, 6, :], dtt[:, 5, :], 1.0 / 17, None, ALU.mult)
                for n in range(15, 1, -2):
                    e.drain()
                    v.scalar_tensor_tensor(dtt[:, 6, :], dtt[:, 6, :], 1.0 / n, dtt[:, 5, :], ALU.add, ALU.mult)
                e.drain()
                v.scalar_tensor_tensor(dtt[:, 6, :], dtt[:, 6, :], 1.0, dtt[:, 4, :], ALU.add, ALU.mult)
                e.drain()
                v.scalar_tensor_tensor(dt16[:, :], dtt[:, 6, :], 2.0, dtt[:, 3, :], ALU.mult, ALU.add)
                e.drain()
                v.tensor_tensor(dtt[:, 7, :].rearrange("p (t h) -> p t h", h=NH),
                                dt16[:, :].rearrange("p (t h) -> p t h", h=NH),
                                arow[:, :].unsqueeze(1).to_broadcast([P, QT, NH]), ALU.mult).then_inc(dt_ready, 1)
                for m in range(CM):
                    e.wait_ge(tap0_done, g * CM + m + 2)
                    for k in range(HALO - 1, -1, -1):
                        ins = v.scalar_tensor_tensor(acc_c[:, m, :], xbc[:, m, k:k + BLK], cw[:, m, k:k + 1],
                                                     acc_c[:, m, :], ALU.mult, ALU.add)
                        if k:
                            e.drain()
                    ins.then_inc(conv_done, 1)
                e.drain()
                v.tensor_copy(xbc[:, :, 0:HALO], xbc[:, :, BLK:BLK + HALO]).then_inc(halo_done, 1)
                f = fill_of("dAT")
                e.wait_ge(filled, n_filled(g, f))
                e.wait_ge(rows_stored, g * 32 + 1)
                v.tensor_copy(dAr[:, :], bank(f)[0:TH, 0:P]).then_inc(dve_emptied, 1)
                e.drain()
                v.tensor_tensor_scan(cumr[:, :], dAr[:, :], zrow[:, :], 1.0, ALU.mult, ALU.add)\
                    .then_inc(cum_ready, 1)
                e.drain()
                v.memset(dAr[:, 0:1], 0.0).then_inc(rows_ready, 1)
                f = fill_of("cumT")
                e.wait_ge(filled, n_filled(g, f))
                v.tensor_copy(cum16[:, :], bank(f)[:, 0:TH]).then_inc(dve_emptied, 1)
                for m in range(CM):
                    e.wait_ge(tanh_done, g * CM + m + 2)
                    v.scalar_tensor_tensor(xc[:, m, :], th[:, m % 2, :], 1.0, acc_c[:, m, :], ALU.add, ALU.mult)\
                        .then_inc(silu_done, 1)
                e.wait_ge(zt_done, g + 2)
                v.scalar_tensor_tensor(zt[:, :, :], zt[:, :, :], 1.0, zh[:, :, :], ALU.add, ALU.mult)\
                    .then_inc(zs_done, 1)
                e.wait_ge(rows_loaded, (g + 1) * 32 + 1)
                for c in range(QT):
                    e.wait_ge(idt_ready, g * QT + c + 2)
                    e.wait_ge(xw_ready, g * QT + c + 1)
                    v.tensor_tensor_scan(lt[:, :, :].rearrange("p h i -> p (h i)"), dAb[:, c * NH * P:(c + 1) * NH * P],
                                         idt[:, c % 2].rearrange("p h i -> p (h i)"), 0.0, ALU.mult, ALU.add)\
                        .then_inc(scan_done, 1)
                    e.drain().then_inc(lt_ready, 1)
                    f = fill_of("cb", c)
                    e.wait_ge(filled, n_filled(g, f))
                    v.tensor_tensor(mt[:, :, :], bank(f)[:, 0:P].unsqueeze(1).to_broadcast([P, NH, P]), lt[:, :, :],
                                    ALU.mult).then_inc(mt_ready, 1)
                    e.drain().then_inc(dve_emptied, 1)
                    f = fill_of("y", c)
                    e.wait_ge(filled, n_filled(g, f))
                    e.wait_ge(xd_ready, g * QT + c + 2)
                    e.wait_ge(y_ready, g * QT + c + 1)
                    v.tensor_tensor(yt[:, 0, :], bank(f)[:, 0:C], xd[:, :], ALU.add)
                    v.tensor_tensor(yt[:, 1, :].rearrange("p (h d) -> p h d", h=NH),
                                    bank(f)[:, C:2 * C].rearrange("p (h d) -> p h d", h=NH),
                                    cum16[:, c * NH:(c + 1) * NH].unsqueeze(2).to_broadcast([P, NH, HD]),
                                    ALU.mult).then_inc(y1_ready, 1)
                    e.drain().then_inc(dve_emptied, 1)
                    f = fill_of("st", c)
                    e.wait_ge(filled, n_filled(g, f))
                    e.wait_ge(Sd_ready, g * QT + c + 2)
                    v.tensor_tensor(S[:, :], bank(f)[:, 0:C], Sd[:, :], ALU.add).then_inc(S_ready, 1)
                    e.drain().then_inc(dve_emptied, 1)
                e.wait_ge(sq_done, (g + 1) * QT + 1)
                rsqrt(ms[:, :], 1.0 / C, 1e-5)
                e.drain()
                for t in range(QT):
                    ins = v.tensor_scalar(x1[:, t, :], y[:, t, :], nw[:, 3, t:t + 1], None, ALU.mult)
                ins.then_inc(yn_ready, 1)
                e.wait_ge(act_emptied, n_emptied(g, fill_of("out", 1)))
                v.tensor_tensor(pools[:, :], pools[:, :], pool1[:, :], ALU.add).then_inc(pool_done, 1)

            v.memset(zrow[:, :], 0.0)
            e.drain()
            with e.Fori(0, B) as b:
                scales(b)
                v.memset(pools[:, :], 0.0)
                v.memset(xbc[:, :, 0:HALO], 0.0).then_inc(halo_done, 1)
                split_projections(b)
                for n in range(KT):
                    max_tile(b * NB, n)
                max_finish(b * NB)
                with e.Fori(0, NB - 1) as i:
                    attention(b * NB + i, True)
                    layer1(b * NB + i)
                attention(b * NB + NB - 1, False)
                layer1(b * NB + NB - 1)
                e.drain()
                v.tensor_scalar(pools[:, :], pools[:, :], 1.0 / N, None, ALU.mult).then_inc(pooled_ready, 1)
                e.wait_ge(gate_th, b + 2)
                v.tensor_scalar(gate[:, :], gate[:, :], 0.5, 0.5, ALU.mult, ALU.add)
                e.drain()
                for n in range(CH * 2):
                    h, cut = n // 2, slice((n % 2) * (N // 2), (n % 2 + 1) * (N // 2))
                    v.scalar_tensor_tensor(img[:, h, cut], img[:, h, cut], gate[:, h:h + 1], x_sb[:, h, cut],
                                           ALU.mult, ALU.add).then_inc(final_done, 1)


def kernel(**inputs):
    import numpy as _np
    import concourse.bacc as _bacc
    from concourse import mybir as _mybir
    from concourse.bass_utils import run_bass_kernel_spmd as _run

    a = {k: _np.asarray(v) for k, v in inputs.items()}
    x = a["x"]
    wqk = _np.concatenate([a["L0_conv_wq"], a["L0_conv_wk"]], 0)
    arrs = {
        "x": x.reshape(x.shape[0], x.shape[1], -1),
        "wqkT": wqk.T, "bqk": _np.concatenate([a["L0_conv_bq"], a["L0_conv_bk"]]),
        "wvT": a["L0_conv_wv"].T, "wv": a["L0_conv_wv"], "gamma": a["L0_conv_gamma"],
        "inT": a["L1_conv_in_w"].T, "wqk": wqk,
        "conv_w": a["L1_conv_conv_w"], "conv_b": a["L1_conv_conv_b"].reshape(-1, P).T,
        "dt_bias": a["L1_conv_dt_bias"], "A_log": a["L1_conv_A_log"], "Dp": a["L1_conv_Dp"],
        "outT": a["L1_conv_out_w"].T, "se1T": a["L1_conv_se1_w"].T, "se1_b": a["L1_conv_se1_b"],
        "se2T": a["L1_conv_se2_w"].T,
        "columns": _np.stack([a[k].reshape(-1, P) for k in ("L1_conv_norm_g", "L1_conv_norm_b", "L1_conv_rms_w",
                                                            "L0_conv_bv", "L1_conv_se2_b")], 0).transpose(2, 0, 1),
    }
    nc = _bacc.Bacc("TRN2", target_bir_lowering=False, num_devices=1)
    arrays, args = {}, []
    for name, v in arrs.items():
        v = _np.ascontiguousarray(v)
        arrays[f"in_{name}_dram"] = v
        args.append(nc.dram_tensor(f"in_{name}_dram", v.shape, _mybir.dt.from_np(v.dtype), kind="ExternalInput").ap())
    shape = arrs["x"].shape
    args.append(nc.dram_tensor("out_0_dram", shape, _mybir.dt.float32, kind="ExternalOutput").ap())
    conv_attention_mamba_kernel(nc, *args)
    r = _run(nc, [arrays], core_ids=[0])
    return r.results[0]["out_0_dram"].reshape(x.shape)
```

```python
from contextlib import ExitStack

import concourse.bass as bass
from concourse import mybir

ALU = mybir.AluOpType
ACT = mybir.ActivationFunctionType
AX = mybir.AxisListType
F32 = mybir.dt.float32
F16 = mybir.dt.float16
I32 = mybir.dt.int32

P = 128
B, C, N = 4, 256, 4096
CH = C // P
D = C // 8
BLK = 512
NB = N // BLK
QT = BLK // P
KT = N // P
KB = N // BLK
NST, HD, NH = 128, 64, 4
CONVD = C + 2 * NST
CM = CONVD // P
TAPS = 4
HALO = TAPS - 1
TH = QT * NH
RING = 4
P32S = 2
PSHIFT = 14 * 0.6931471805599453
MROW = 256.0
STK = 3 * D
VW = C + 2
EXPMASK = 0x7F800000
ONEBITS = 127 << 23

FILLS = ([("xT", 0)] * 2 + [("x1T", 0)] * 2 + [("uT", 0)] * 2 + [("dt", 1)] + [("xbc", 0)] * CM
         + [("z", 0)] * 2 + [("dAT", 1), ("cumT", 1)] + [("xsB", 0)] * QT
         + [("cb", 1), ("y", 1), ("st", 1)] * QT + [("yT", 0)] * 2 + [("out", 0)] * 2)
NF = len(FILLS)
FIRST = {}
for _n, (_name, _e) in enumerate(FILLS):
    FIRST.setdefault(_name, _n)
PER_EMPTIER = [sum(1 for _, e in FILLS if e == who) for who in (0, 1)]


AT_NORM, AT_X1T, AT_UT, AT_DT = 0, 1, 3, 4
AT_XBC, AT_Z, AT_DAT, AT_CUM = 5, 9, 10, 11
AT_XSB = 12
AT_CHUNK, CHUNK_STEPS = 13, 3
AT_RMS, AT_YT, AT_OUT = 27, 29, 30

NO_MAX, TWO_MAX = (0, 6, KT - 2, KT - 1), (3, 4, 26, 29)
MAX_TILES, _n = [], 0
for _k in range(KT):
    _m = 0 if _k in NO_MAX else 2 if _k in TWO_MAX else 1
    MAX_TILES.append(list(range(_n, _n + _m)))
    _n += _m
assert _n == KT
LOW_NORM, LOW_CONV, LOW_RMS = (1, 2, 3), range(7, 13), (28, 29, 30)
LOW_CHUNK = [AT_CHUNK + CHUNK_STEPS * (_c + 1) + 1 for _c in range(QT)]
POOL_LOW = [*LOW_NORM, *LOW_CONV, *LOW_CHUNK, *LOW_RMS]


def fill_of(name, k=0):
    return FIRST[name] + (3 * k if name in ("cb", "y", "st") else k)


def emptied_count(f):
    return sum(1 for _, e in FILLS[:f + 1] if e == FILLS[f][1])


def conv_attention_mamba_kernel(nc, x, wqkT, bqk, wvT, wv, gamma, inT, wqk, conv_w, conv_b,
                                dt_bias, A_log, Dp, outT, se1T, se1_b, se2T, columns, out):
    ctx = ExitStack()
    with ctx:
        def sb(name, shape, dt=F32):
            return ctx.enter_context(nc.sbuf_tensor(name, shape, dt))

        def ps(name):
            return ctx.enter_context(nc.psum_tensor(name, [P, 512], F32))

        def sem(name):
            return ctx.enter_context(nc.semaphore(name))

        x_sb = sb("x_sb", [P, CH, N])
        img = sb("img", [P, CH, N])
        v_hi = sb("v_hi", [P, KT, VW], F16)
        v_lo = sb("v_lo", [P, KT, VW], F16)
        qk_hi = sb("qk_hi", [2 * D, BLK], F16)
        qk_lo = sb("qk_lo", [2 * D, BLK], F16)
        kstack = sb("kstack", [STK + 2, N], F16)
        q_next = sb("q_next", [STK + 2, BLK], F16)
        q_cur = sb("q_cur", [STK + 2, BLK], F16)
        wqkT_sb = sb("wqkT_sb", [P, CH, 2 * D])
        wvT_sb = sb("wvT_sb", [P, CH, C])
        inT_sb = sb("inT_sb", [P, CH, 2 * C + 2 * NST + NH])
        outT_sb = sb("outT_sb", [P, CH, C])
        se1T_sb = sb("se1T_sb", [P, CH, C // 4])
        se2T_sb = sb("se2T_sb", [C // 4, C])
        cols = sb("cols", [P, 5, CH])
        gcol, bcol, rmscol, bvcol, s2col = (cols[:, k, :] for k in range(5))
        se1b = sb("se1b", [C // 4, 1])
        cw = sb("cw", [P, CM, TAPS])
        cb = sb("cb", [P, CM])
        bqk_sb = sb("bqk_sb", [2 * D, 1])
        gam = sb("gam", [P, 1])
        gbv = sb("gbv", [P, CH])
        dtb = sb("dtb", [P, NH])
        alog = sb("alog", [P, NH])
        arow = sb("arow", [P, NH])
        dcol = sb("dcol", [P, NH])
        ident = sb("ident", [P, P])
        identh = sb("identh", [P, P], F16)
        zrow = sb("zrow", [TH, P])
        wnat = img[:, 0, 0:4 * C]
        wmax = sb("wmax", [P, 5])
        wmaxa = sb("wmaxa", [P, 5])
        xmax = sb("xmax", [P, CH * 2])
        xmaxa = sb("xmaxa", [P, CH * 2])
        sc = sb("sc", [P, 8])
        sci = sb("sci", [P, 8], I32)
        qkscale = sb("qkscale", [2 * D, 1])
        xp = sb("xp", [P, 2, CH, BLK])
        qkf = sb("qkf", [2 * D, BLK])
        p32 = sb("p32", [P, P32S, BLK])
        p_hi = sb("p_hi", [P, RING, BLK], F16)
        p_lo = sb("p_lo", [P, RING, BLK], F16)
        maxes = sb("maxes", [P, QT, KB])
        mcol = sb("mcol", [P, 2, QT])
        mparts = sb("mparts", [P, QT, 2], F16)
        xb = xp[:, 0]
        shared = sb("shared", [P, 2, QT * C])
        xT = shared[:, 1, :].rearrange("p (t c) -> p t c", t=QT)
        uT = shared[:, 0, :].rearrange("p (h n) -> p h n", h=CH)
        yT = shared[:, 1, :].rearrange("p (h n) -> p h n", h=CH)
        dAb = shared[:, :, :].rearrange("p a n -> p (a n)")
        x1 = sb("x1", [P, QT, C])
        rden = sb("rden", [P, 2, QT])
        bst = sb("bst", [P, QT, 6])
        mv = sb("mv", [P, QT, 2])
        nw = sb("nw", [P, 4, QT])
        nwi = nw[:, :, :].bitcast(I32)
        xbc = sb("xbc", [P, CM, HALO + BLK])
        acc_c = sb("acc_c", [P, CM, BLK])
        th = xp[:, 1]
        zh = sb("zh", [P, QT, C])
        zt = sb("zt", [P, QT, C])
        dtt = sb("dtt", [P, 8, TH])
        dt16 = sb("dt16", [P, TH])
        dA16 = sb("dA16", [P, TH])
        cum16 = sb("cum16", [P, TH])
        dAr = sb("dAr", [TH, P])
        cumr = sb("cumr", [TH, P])
        totb = sb("totb", [P, TH])
        idt = sb("idt", [P, 2, NH, P])
        lt = sb("lt", [P, NH, P])
        mt = sb("mt", [P, NH, P])
        xsB = sb("xsB", [P, QT, C + NST])
        xd = sb("xd", [P, C])
        xw = sb("xw", [P, C])
        S = sb("S", [P, C])
        Sd = sb("Sd", [P, C])
        yt = sb("yt", [P, 2, C])
        y = sb("y", [P, QT, C])
        ms = sb("ms", [P, QT])
        pool1 = sb("pool1", [P, CH])
        pools = sb("pools", [P, CH])
        hdn = sb("hdn", [C // 4, 1])
        gate = sb("gate", [P, CH])
        u = y
        xc = acc_c

        acc = [ps(f"acc{t}") for t in range(QT)]
        p_et, p_mx = ps("p_et"), ps("p_mx")
        pl = [ps("pl0"), ps("pl1")]

        rows_d = nc.dram_tensor("rows_d", (TH * P,), F32, kind="Internal").ap()
        hi_d = nc.dram_tensor("hi_d", (2 * D, N), F16, kind="Internal").ap()
        lo_d = nc.dram_tensor("lo_d", (2 * D, N), F16, kind="Internal").ap()
        tot_d = nc.dram_tensor("tot_d", (TH,), F32, kind="Internal").ap()

        w_loaded = sem("w_loaded")
        ident_ready = sem("ident_ready")
        consts_ready = sem("consts_ready")
        wmax_ready = sem("wmax_ready")
        wmax_all = sem("wmax_all")
        prep_done = sem("prep_done")
        x_loaded = [sem(f"x_loaded{n}") for n in range(CH * 2)]
        xmax_ready = sem("xmax_ready")
        xmax_all = sem("xmax_all")
        scales_ready = sem("scales_ready")
        xp_ready = sem("xp_ready")
        qk_filled = sem("qk_filled")
        qk_emptied = sem("qk_emptied")
        v_filled = sem("v_filled")
        v_hi_done = sem("v_hi_done")
        v_lo_done = sem("v_lo_done")
        qk_stored = sem("qk_stored")
        k_loaded = sem("k_loaded")
        q_loaded = sem("q_loaded")
        mx_ready = sem("mx_ready")
        max_done = sem("max_done")
        m_ready = sem("m_ready")
        m_filled = sem("m_filled")
        q_next_done = sem("q_next_done")
        q_cur_ready = sem("q_cur_ready")
        et_ready = sem("et_ready")
        exp_done = sem("exp_done")
        hi_done = sem("hi_done")
        lo_done = sem("lo_done")
        pv_done = sem("pv_done")
        x1_done = sem("x1_done")
        xb_ready = sem("xb_ready")
        filled = sem("filled")
        act_emptied = sem("act_emptied")
        dve_emptied = sem("dve_emptied")
        u_ready = sem("u_ready")
        halo_done = sem("halo_done")
        tap0_done = sem("tap0_done")
        conv_done = sem("conv_done")
        tanh_done = sem("tanh_done")
        silu_done = sem("silu_done")
        zt_done = sem("zt_done")
        zs_done = sem("zs_done")
        dtabs_ready = sem("dtabs_ready")
        dtexp_done = sem("dtexp_done")
        dt_ready = sem("dt_ready")
        dA_done = sem("dA_done")
        rows_ready = sem("rows_ready")
        cum_ready = sem("cum_ready")
        rows_stored = sem("rows_stored")
        rows_loaded = sem("rows_loaded")
        idt_ready = sem("idt_ready")
        lt_ready = sem("lt_ready")
        mt_ready = sem("mt_ready")
        xd_ready = sem("xd_ready")
        xw_ready = sem("xw_ready")
        Sd_ready = sem("Sd_ready")
        S_ready = sem("S_ready")
        y1_ready = sem("y1_ready")
        y_ready = sem("y_ready")
        sq_done = sem("sq_done")
        yn_ready = sem("yn_ready")
        pool_done = sem("pool_done")
        state_zero = sem("state_zero")
        pooled_ready = sem("pooled_ready")
        se1_filled = sem("se1_filled")
        hdn_ready = sem("hdn_ready")
        se2_filled = sem("se2_filled")
        gate_th = sem("gate_th")
        gate_ready = sem("gate_ready")
        final_done = sem("final_done")
        out_stored = sem("out_stored")
        scan_done = sem("scan_done")
        settled = sem("settled")
        from_one = [ident_ready, consts_ready, wmax_ready, wmax_all, prep_done,
                    *x_loaded, xmax_ready, xmax_all, scales_ready, xp_ready, qk_filled,
                    qk_emptied, v_filled, v_hi_done, v_lo_done, qk_stored, k_loaded,
                    q_loaded, mx_ready, max_done, m_ready, m_filled, q_next_done,
                    q_cur_ready, et_ready, exp_done, hi_done, lo_done, pv_done,
                    x1_done, xb_ready, filled, act_emptied, dve_emptied, u_ready,
                    halo_done, tap0_done, conv_done, tanh_done, silu_done, zt_done,
                    zs_done, dtabs_ready, dtexp_done, dt_ready, dA_done, rows_ready,
                    cum_ready, rows_stored, rows_loaded, idt_ready, lt_ready, mt_ready,
                    xd_ready, xw_ready, Sd_ready, S_ready, y1_ready, y_ready,
                    sq_done, yn_ready, pool_done, state_zero, pooled_ready, se1_filled,
                    hdn_ready, se2_filled, gate_th, gate_ready, final_done, out_stored,
                    scan_done, settled]

        xv = x.rearrange("b (h p) n -> b p h n", p=P)
        ov = out.rearrange("b (h p) n -> b p h n", p=P)
        block = ctx.enter_context(nc.Block())

        def n_emptied(g, f):
            return g * PER_EMPTIER[FILLS[f][1]] + emptied_count(f) + 1

        def n_filled(g, f):
            return g * NF + f + 2

        def bank(f):
            return pl[f % 2]

        def settle(e):
            e.sem_inc(settled, 1)

        @block.sync
        def _(e):
            def batch_start(b):
                with e.Fori(0, NB) as j:
                    e.wait_ge(qk_emptied, b * NB + j + 2)
                    settle(e)
                    for dst, src in ((hi_d, qk_hi), (lo_d, qk_lo)):
                        e.dma_start(dst[:, bass.ds(j * BLK, BLK)], src[:, :]).then_inc(qk_stored, 16)
                e.wait_ge(qk_stored, (b + 1) * NB * 32 + 1)
                e.wait_ge(et_ready, b * NB * KT + 1)
                settle(e)
                for src, row in ((hi_d, 0), (lo_d, D), (hi_d, 2 * D)):
                    e.dma_start(kstack[row:row + D, :], src[D:2 * D, :]).then_inc(k_loaded, 16)

            def load_q(g, i):
                e.wait_ge(q_cur_ready, g + 1)
                settle(e)
                for src, row in ((hi_d, 0), (hi_d, D), (lo_d, 2 * D)):
                    e.dma_start(q_next[row:row + D, :], src[0:D, bass.ds(i * BLK, BLK)])\
                        .then_inc(q_loaded, 16)

            def decay_rows(g):
                e.wait_ge(rows_ready, g + 2)
                e.dma_start(rows_d.rearrange("(r i) -> r i", i=P), dAr[:, :]).then_inc(rows_stored, 16)
                e.wait_ge(cum_ready, g + 2)
                e.dma_start(tot_d.rearrange("(r a) -> r a", a=1), cumr[:, P - 1:P]).then_inc(rows_stored, 16)
                e.wait_ge(rows_stored, (g + 1) * 32 + 1)
                e.wait_ge(filled, g * NF + fill_of("z", 1) + 2)
                settle(e)
                e.wait_ge(scan_done, g * QT + 1)
                e.wait_ge(Sd_ready, g * QT + 1)
                e.dma_start(dAb, rows_d.partition_broadcast(P)).then_inc(rows_loaded, 16)
                e.dma_start(totb[:, :], tot_d.partition_broadcast(P)).then_inc(rows_loaded, 16)

            def load_x(b, n):
                h, half = n // 2, n % 2
                e.dma_start(x_sb[:, h, half * (N // 2):(half + 1) * (N // 2)],
                            xv[b, :, h, half * (N // 2):(half + 1) * (N // 2)]).then_inc(x_loaded[n], 16)

            def batch(b, more):
                batch_start(b)
                load_q(b * NB, 0)
                load_q(b * NB + 1, 1)
                with e.Fori(1, NB - 1) as i:
                    load_q(b * NB + i + 1, i + 1)
                    decay_rows(b * NB + i - 1)
                decay_rows(b * NB + NB - 2)
                decay_rows(b * NB + NB - 1)
                for n in range(CH * 2):
                    h, half = n // 2, n % 2
                    e.wait_ge(final_done, b * CH * 2 + n + 2)
                    settle(e)
                    if more:
                        load_x(b + 1, n)
                    e.dma_start(ov[b, :, h, half * (N // 2):(half + 1) * (N // 2)],
                                img[:, h, half * (N // 2):(half + 1) * (N // 2)]).then_inc(out_stored, 16)

            for n in range(CH * 2):
                load_x(0, n)
            with e.Fori(0, B - 1) as b:
                batch(b, True)
            batch(B - 1, False)
            e.wait_ge(out_stored, B * CH * 2 * 16 + 1)

        @block.gpsimd
        def _(e):
            for semaphore in from_one:
                e.sem_inc(semaphore, 1)
            e.memset(wnat, 0.0)
            e.memset(wmax[:, :], 0.0)
            e.drain()
            wdmas = [(wqkT_sb[:, :, :], wqkT.rearrange("(h p) n -> p h n", p=P)),
                     (wvT_sb[:, :, :], wvT.rearrange("(h p) n -> p h n", p=P)),
                     (inT_sb[:, :, :], inT.rearrange("(h p) n -> p h n", p=P)),
                     (outT_sb[:, :, :], outT.rearrange("(h p) n -> p h n", p=P)),
                     (se1T_sb[:, :, :], se1T.rearrange("(h p) n -> p h n", p=P)),
                     (se2T_sb[:, :], se2T),
                     (cw[:, :, :], conv_w.rearrange("(m p) k -> p m k", p=P)),
                     (cb[:, :], conv_b),
                     (bqk_sb[:, :], bqk.rearrange("(p a) -> p a", a=1)),
                     (se1b[:, :], se1_b.rearrange("(p a) -> p a", a=1)),
                     (gam[:, :], gamma.partition_broadcast(P)),
                     (dtb[:, :], dt_bias.partition_broadcast(P)),
                     (alog[:, :], A_log.partition_broadcast(P)),
                     (dcol[:, :], Dp.partition_broadcast(P)),
                     (wnat[:, 0:2 * C].rearrange("p (h n) -> p h n", h=2), wv.rearrange("(h p) n -> p h n", p=P)),
                     (wnat[0:D, 2 * C:3 * C], wqk[0:D, :]),
                     (wnat[0:D, 3 * C:4 * C], wqk[D:2 * D, :]),
                     (wmax[0:D, 3:4], bqk[0:D].rearrange("(p a) -> p a", a=1)),
                     (wmax[0:D, 4:5], bqk[D:2 * D].rearrange("(p a) -> p a", a=1))]
            wdmas.append((cols[:, :, :], columns))
            for dst, src in wdmas:
                e.dma_start(dst, src).then_inc(w_loaded, 16)
            e.memset(ident[:, :], 0.0)
            e.memset(identh[:, :], 0.0)
            e.drain()
            e.memset(kstack[STK:STK + 2, :], -MROW)
            e.drain()
            for m in (ident, identh):
                e.affine_select(out=m[:, :], in_=m[:, :], compare_op=ALU.not_equal, fill=1.0, base=0,
                                pattern=[[-1, P]], channel_multiplier=1)
            e.drain().then_inc(ident_ready, 1)
            e.wait_ge(w_loaded, 16 * len(wdmas))
            e.drain().then_inc(consts_ready, 1)
            e.wait_ge(wmax_ready, 2)
            e.partition_all_reduce(wmaxa[:, :], wmax[:, :], P, bass.bass_isa.ReduceOp.absmax).then_inc(wmax_all, 1)

            def batch_start(b):
                e.wait_ge(xmax_ready, b + 2)
                settle(e)
                e.partition_all_reduce(xmaxa[:, :], xmax[:, :], P, bass.bass_isa.ReduceOp.max).then_inc(xmax_all, 1)
                e.wait_ge(filled, b * NB * NF + 1)
                settle(e)
                e.memset(S[:, :], 0.0).then_inc(state_zero, 1)
                for j in range(2):
                    e.tensor_copy(xp[:, j, :, :], x_sb[:, :, j * BLK:(j + 1) * BLK]).then_inc(xp_ready, 1)
                with e.Fori(1, NB // 2) as jj:
                    for r in range(2):
                        j = jj * 2 + r
                        e.wait_ge(v_filled, b * NB * 2 + j * 2 - 2 + 1)
                        settle(e)
                        e.tensor_copy(xp[:, r, :, :], x_sb[:, :, bass.ds(j * BLK, BLK)]).then_inc(xp_ready, 1)

            def source_weights(g, c):
                e.wait_ge(scan_done, g * QT + max(c - 1, 0) + 1)
                e.tensor_tensor(idt[:, c % 2], ident[:, :].unsqueeze(1).to_broadcast([P, NH, P]),
                                dt16[:, c * NH:(c + 1) * NH].unsqueeze(2).to_broadcast([P, NH, P]),
                                ALU.mult).then_inc(idt_ready, 1)

            def skip_product(g, c):
                e.wait_ge(act_emptied, n_emptied(g, fill_of("xsB", c)))
                e.wait_ge(y1_ready, g * QT + c + 1)
                e.tensor_tensor(xd[:, :].rearrange("p (h d) -> p h d", h=NH),
                                xsB[:, c, 0:C].rearrange("p (h d) -> p h d", h=NH),
                                dcol[:, :].unsqueeze(2).to_broadcast([P, NH, HD]), ALU.mult).then_inc(xd_ready, 1)

            def lo_tile(g, k):
                e.wait_ge(hi_done, g * KT + k + 2)
                e.wait_ge(pv_done, g * KT + k + 2)
                e.wait_ge(lo_done, g * KT + k + P32S + 1)
                e.tensor_tensor(p_lo[:, k % RING, :], p32[:, k % P32S, :], p_hi[:, k % RING, :],
                                ALU.subtract).then_inc(lo_done, 1)

            def layer1(g, more):
                if more:
                    for k in LOW_NORM:
                        lo_tile(g + 1, k)
                for m in range(CM):
                    if more and m:
                        lo_tile(g + 1, LOW_CONV[m - 1])
                    e.wait_ge(act_emptied, n_emptied(g, fill_of("xbc", m)))
                    e.wait_ge(filled, g * NF + 1)
                    settle(e)
                    e.tensor_scalar(acc_c[:, m, :], xbc[:, m, HALO:HALO + BLK], cw[:, m, HALO:TAPS], cb[:, m:m + 1],
                                    ALU.mult, ALU.add).then_inc(tap0_done, 1)
                if more:
                    for k in LOW_CONV[CM - 1:]:
                        lo_tile(g + 1, k)
                e.wait_ge(dt_ready, g + 2)
                source_weights(g, 0)
                skip_product(g, 0)
                for c in range(QT):
                    e.wait_ge(lt_ready, g * QT + c + 2)
                    e.wait_ge(S_ready, g * QT + c + 1)
                    e.tensor_tensor(xw[:, :].rearrange("p (h d) -> p h d", h=NH),
                                    xsB[:, c, 0:C].rearrange("p (h d) -> p h d", h=NH),
                                    lt[:, :, P - 1:P].to_broadcast([P, NH, HD]), ALU.mult).then_inc(xw_ready, 1)
                    e.wait_ge(rows_loaded, (g + 1) * 32 + 1)
                    e.tensor_tensor(Sd[:, :].rearrange("p (h d) -> p h d", h=NH),
                                    S[:, :].rearrange("p (h d) -> p h d", h=NH),
                                    totb[:, c * NH:(c + 1) * NH].unsqueeze(2).to_broadcast([P, NH, HD]),
                                    ALU.mult).then_inc(Sd_ready, 1)
                    if c + 1 < QT:
                        source_weights(g, c + 1)
                    if more:
                        lo_tile(g + 1, LOW_CHUNK[c])
                    e.wait_ge(y1_ready, g * QT + c + 2)
                    e.wait_ge(zs_done, g + 2)
                    e.tensor_tensor(yt[:, 0, :], yt[:, 0, :], yt[:, 1, :], ALU.add)
                    e.drain()
                    e.tensor_tensor(y[:, c, :], yt[:, 0, :], zt[:, c, :], ALU.mult).then_inc(y_ready, 1)
                    if c + 1 < QT:
                        skip_product(g, c + 1)
                if more:
                    for k in LOW_RMS:
                        lo_tile(g + 1, k)

            with e.Fori(0, B) as b:
                batch_start(b)
                with e.Fori(0, NB - 1) as i:
                    layer1(b * NB + i, True)
                layer1(b * NB + NB - 1, False)

        @block.scalar
        def _(e):
            e.wait_ge(wmax_ready, 2)
            e.activation(arow[:, :], alog[:, :], ACT.Exp).then_inc(prep_done, 1)

            def batch_start(b):
                e.wait_ge(scales_ready, b + 2)
                e.wait_ge(pv_done, b * NB * KT + RING + 1)
                settle(e)
                with e.Fori(0, NB) as j:
                    for t in range(2):
                        e.wait_ge(v_filled, b * NB * 2 + j * 2 + t + 2)
                        settle(e)
                        e.activation(v_hi[:, bass.ds(j * 4 + t * 2, 2), 0:C],
                                     pl[t][:, :].rearrange("p (n c) -> p n c", n=2), ACT.Copy,
                                     scale=sc[:, 0:1]).then_inc(v_hi_done, 1)

            def exp_tile(g, k):
                e.wait_ge(et_ready, g * KT + k + 2)
                e.wait_ge(lo_done, g * KT + k + 2)
                e.activation(p32[:, k % P32S, :], p_et[:, :], ACT.Exp).then_inc(exp_done, 1)

            def hi_tile(g, k):
                e.wait_ge(exp_done, g * KT + k + 2)
                e.wait_ge(pv_done, g * KT + k + 2)
                e.activation(p_hi[:, k % RING, :], p32[:, k % P32S, :], ACT.Copy).then_inc(hi_done, 1)

            def attention(g, i, more, behind):
                for k in range(KT):
                    if k + 1 < KT:
                        hi_tile(g, k + 1)
                    if k + 2 < KT:
                        exp_tile(g, k + 2)
                    if behind:
                        layer1(g - 1, i - 1, k)
                residual(g, i, more)

            def residual(g, i, more):
                e.wait_ge(filled, g * NF + 1)
                settle(e)
                for h in range(CH):
                    e.activation(xb[:, h, :], x_sb[:, h, bass.ds(i * BLK, BLK)], ACT.Identity,
                                 bias=gbv[:, h:h + 1]).then_inc(xb_ready, 1)
                if more:
                    exp_tile(g + 1, 0)
                    hi_tile(g + 1, 0)
                for k in range(2):
                    if more and k == 1:
                        exp_tile(g + 1, 1)
                    f = fill_of("xT", k)
                    e.wait_ge(filled, n_filled(g, f))
                    e.wait_ge(x1_done, (g + 1) * QT + 1)
                    e.activation(xT[:, 2 * k:2 * k + 2, :], bank(f)[:, :].rearrange("p (t c) -> p t c", t=2),
                                 ACT.Copy).then_inc(act_emptied, 1)

            def layer1(g, i, k):
                if AT_X1T <= k < AT_X1T + CH:
                    h = k - AT_X1T
                    f = fill_of("x1T", h)
                    e.wait_ge(filled, n_filled(g, f))
                    settle(e)
                    e.activation(x_sb[:, h, bass.ds(i * BLK, BLK)], bank(f)[:, :], ACT.Copy).then_inc(act_emptied, 1)
                if k == AT_UT:
                    for h in range(CH):
                        f = fill_of("uT", h)
                        e.wait_ge(filled, n_filled(g, f))
                        e.activation(uT[:, h, :], bank(f)[:, :], ACT.Identity, bias=bcol[:, h:h + 1],
                                     scale=gcol[:, h:h + 1]).then_inc(act_emptied, 1)
                if k == AT_DT:
                    e.wait_ge(dtabs_ready, g + 2)
                    e.activation(dtt[:, 2, :], dtt[:, 1, :], ACT.Exp, scale=-1.0).then_inc(dtexp_done, 1)
                if AT_XBC <= k < AT_XBC + CM:
                    m = k - AT_XBC
                    f = fill_of("xbc", m)
                    e.wait_ge(filled, n_filled(g, f))
                    if m == 0:
                        e.wait_ge(halo_done, halo_count(g) + 1)
                    e.activation(xbc[:, m, HALO:HALO + BLK], bank(f)[:, :], ACT.Copy).then_inc(act_emptied, 1)
                if k == AT_XBC + 3:
                    e.wait_ge(dt_ready, g + 2)
                    e.activation(dA16[:, :], dtt[:, 7, :], ACT.Exp).then_inc(dA_done, 1)
                if AT_XBC + 2 <= k < AT_XBC + 2 + CM:
                    m = k - AT_XBC - 2
                    e.wait_ge(conv_done, g * CM + m + 2)
                    e.wait_ge(silu_done, g * CM + max(m - 1, 0) + 1)
                    e.activation(th[:, m % 2, :], acc_c[:, m, :], ACT.Tanh).then_inc(tanh_done, 1)
                if AT_Z <= k < AT_Z + 2:
                    r = k - AT_Z
                    f = fill_of("z", r)
                    e.wait_ge(filled, n_filled(g, f))
                    e.wait_ge(y_ready, g * QT + 1)
                    e.activation(zh[:, 2 * r:2 * r + 2, :], bank(f)[:, :].rearrange("p (t c) -> p t c", t=2),
                                 ACT.Copy, scale=0.5).then_inc(act_emptied, 1)
                if k == AT_Z + 1:
                    e.wait_ge(act_emptied, n_emptied(g, fill_of("z", 1)))
                    e.activation(zt[:, :, :], zh[:, :, :], ACT.Tanh).then_inc(zt_done, 1)
                if AT_XSB <= k < AT_XSB + 2:
                    for c in range(2 * (k - AT_XSB), 2 * (k - AT_XSB) + 2):
                        f = fill_of("xsB", c)
                        e.wait_ge(filled, n_filled(g, f))
                        e.activation(xsB[:, c, :], bank(f)[:, 0:C + NST], ACT.Copy).then_inc(act_emptied, 1)
                for c in range(QT):
                    if k == AT_CHUNK + CHUNK_STEPS * (c + 1) + 1:
                        e.wait_ge(y_ready, g * QT + c + 2)
                        e.activation(x1[:, c, :], y[:, c, :], ACT.Square, accum_out=ms[:, c:c + 1])\
                            .then_inc(sq_done, 1)
                if k == AT_YT:
                    for h in range(CH):
                        f = fill_of("yT", h)
                        e.wait_ge(filled, n_filled(g, f))
                        e.activation(yT[:, h, :], bank(f)[:, :], ACT.Copy, scale=rmscol[:, h:h + 1])\
                            .then_inc(act_emptied, 1)
                if k == AT_OUT:
                    for h in range(CH):
                        f = fill_of("out", h)
                        e.wait_ge(filled, n_filled(g, f))
                        e.wait_ge(pool_done, g + 1)
                        e.wait_ge(out_stored, stored_count(g) + 1)
                        settle(e)
                        e.activation(img[:, h, bass.ds(i * BLK, BLK)], bank(f)[:, :], ACT.Copy,
                                     accum_out=pool1[:, h:h + 1]).then_inc(act_emptied, 1)

            with e.Fori(0, B) as b:
                batch_start(b)

                def halo_count(g):
                    return g + b + 1

                def stored_count(g):
                    return b * CH * 2 * 16

                exp_tile(b * NB, 0)
                hi_tile(b * NB, 0)
                exp_tile(b * NB, 1)
                attention(b * NB, 0, True, False)
                with e.Fori(1, NB - 1) as i:
                    attention(b * NB + i, i, True, True)
                attention(b * NB + NB - 1, NB - 1, False, True)
                for k in range(KT):
                    layer1(b * NB + NB - 1, NB - 1, k)
                e.wait_ge(se1_filled, b + 2)
                e.activation(hdn[:, :], pl[0][0:C // 4, 0:1], ACT.Relu, bias=se1b[:, :]).then_inc(hdn_ready, 1)
                e.wait_ge(se2_filled, b + 2)
                for h in range(CH):
                    e.activation(gate[:, h:h + 1], pl[1][:, h:h + 1], ACT.Identity, bias=s2col[:, h:h + 1])
                e.drain()
                e.activation(gate[:, :], gate[:, :], ACT.Tanh, scale=0.5).then_inc(gate_th, 1)

        @block.tensor
        def _(e):
            e.wait_ge(ident_ready, 2)
            e.wait_ge(consts_ready, 2)
            e.sem_inc(pv_done, RING)
            e.sem_inc(x1_done, QT)

            def projections(b):
                e.wait_ge(exp_done, b * NB * KT + 1)
                e.wait_ge(act_emptied, b * NB * PER_EMPTIER[0] + 1)
                e.wait_ge(gate_th, b + 1)
                settle(e)
                with e.Fori(0, NB // 2) as jj:
                    for r in range(2):
                        j = jj * 2 + r
                        e.wait_ge(xp_ready, b * NB + j + 2)
                        e.wait_ge(qk_emptied, b * NB + j + 1)
                        for h in range(CH):
                            mm = e.matmul(p_et[0:2 * D, :], wqkT_sb[:, h, :], xp[:, r, h, :],
                                          start=(h == 0), stop=(h == CH - 1))
                        mm.then_inc(qk_filled, 1)
                        for t in range(2):
                            e.wait_ge(v_lo_done, b * NB * 2 + j * 2 + t - (1 if t else 0) + 1)
                            for k in range(2):
                                tok = (2 * t + k) * P
                                for h in range(CH):
                                    mm = e.matmul(pl[t][:, k * C:(k + 1) * C], xp[:, r, h, tok:tok + P],
                                                  wvT_sb[:, h, :], start=(h == 0), stop=(h == CH - 1))
                            mm.then_inc(v_filled, 1)

            def max_tile(g, n, banks):
                e.wait_ge(max_done, g * KT + max(n + 1 - len(banks), 0) + 1)
                if n == 0:
                    e.wait_ge(q_loaded, (g + 1) * 48 + 1)
                    e.wait_ge(q_next_done, g + 1)
                q, kb = n // KB, n % KB
                e.matmul(banks[n % len(banks)][:, :], q_next[0:STK, q * P:(q + 1) * P], kstack[0:STK, kb * BLK:(kb + 1) * BLK],
                         start=True, stop=True).then_inc(mx_ready, 1)

            def max_rows(g):
                e.wait_ge(m_ready, g + 2)
                for t in range(QT):
                    mm = e.matmul(p_mx[STK:STK + 2, t * P:(t + 1) * P], mparts[:, t, :], identh[:, :],
                                  start=True, stop=True)
                mm.then_inc(m_filled, 1)

            def energies(g, k):
                e.wait_ge(exp_done, g * KT + k + 1)
                e.matmul(p_et[:, :], kstack[:, k * P:(k + 1) * P], q_cur[:, :],
                         start=True, stop=True).then_inc(et_ready, 1)

            def values(g, k):
                e.wait_ge(hi_done, g * KT + k + 2)
                r = k % RING
                for t in range(QT):
                    if k == 0:
                        e.wait_ge(x1_done, g * QT + t + 2)
                    e.matmul(acc[t][:, 0:C + 1], p_hi[:, r, t * P:(t + 1) * P], v_hi[:, k, 0:C + 1],
                             start=(k == 0), stop=False)
                    e.matmul(acc[t][:, 0:C], p_hi[:, r, t * P:(t + 1) * P], v_lo[:, k, 0:C],
                             start=False, stop=False, skip_group_check=True)
                e.wait_ge(lo_done, g * KT + k + 1 + P32S + 1)
                for t in range(QT):
                    mm = e.matmul(acc[t][:, 0:C + 1], p_lo[:, r, t * P:(t + 1) * P], v_hi[:, k, 0:C + 1],
                                  start=False, stop=(k == KT - 1))
                mm.then_inc(pv_done, 1)

            def attention(g, more, behind):
                for k in range(KT):
                    if k + 2 < KT:
                        energies(g, k + 2)
                    if more:
                        for n in MAX_TILES[k][:1]:
                            max_tile(g + 1, n, [p_mx])
                        if k == KT - 1:
                            max_rows(g + 1)
                    if behind:
                        layer1_early(g - 1, k)
                    values(g, k)
                    if more:
                        for n in MAX_TILES[k][1:]:
                            max_tile(g + 1, n, [p_mx])
                    if behind:
                        layer1(g - 1, k)
                if more:
                    first_energies(g + 1)
                residual(g, more)

            def first_energies(g):
                e.wait_ge(q_cur_ready, g + 2)
                energies(g, 0)

            def begin(g, f):
                if f >= 2:
                    e.wait_ge(dve_emptied if FILLS[f - 2][1] else act_emptied, n_emptied(g, f - 2))
                else:
                    e.wait_ge(act_emptied, g * PER_EMPTIER[0] + 1)
                return bank(f)

            def residual(g, more):
                for k in range(2):
                    if more and k == 1:
                        energies(g + 1, 1)
                    f = fill_of("xT", k)
                    o = begin(g, f)
                    e.wait_ge(xb_ready, (g + 1) * CH + 1)
                    for t in range(2):
                        for h in range(CH):
                            mm = e.transpose(o[:, t * C + h * P:t * C + (h + 1) * P],
                                             xb[:, h, (2 * k + t) * P:(2 * k + t + 1) * P], ident[:, :])
                    mm.then_inc(filled, 1)

            def turn(g, f, src, h):
                o = begin(g, f)
                for t in range(QT):
                    mm = e.transpose(o[:, t * P:(t + 1) * P], src[:, t, h * P:(h + 1) * P], ident[:, :])
                mm.then_inc(filled, 1)

            def layer1_early(g, k):
                for c in range(QT):
                    if k == AT_CHUNK + CHUNK_STEPS * c + 1:
                        f = fill_of("cb", c)
                        o = begin(g, f)
                        e.matmul(o[:, 0:P], xc[:, 2, c * P:(c + 1) * P], xc[:, 3, c * P:(c + 1) * P],
                                 start=True, stop=True).then_inc(filled, 1)

            def layer1(g, k):
                if AT_X1T <= k < AT_X1T + CH:
                    e.wait_ge(x1_done, (g + 2) * QT + 1)
                    turn(g, fill_of("x1T", k - AT_X1T), x1, k - AT_X1T)
                if k == AT_UT:
                    e.wait_ge(u_ready, g + 2)
                    for h in range(CH):
                        turn(g, fill_of("uT", h), u, h)
                if k == AT_DT:
                    e.wait_ge(act_emptied, n_emptied(g, fill_of("uT", 1)))
                    f = fill_of("dt")
                    o = begin(g, f)
                    for t in range(QT):
                        for h in range(CH):
                            mm = e.matmul(o[:, t * NH:(t + 1) * NH], uT[:, h, t * P:(t + 1) * P],
                                          inT_sb[:, h, C + CONVD:C + CONVD + NH], start=(h == 0), stop=(h == CH - 1))
                    mm.then_inc(filled, 1)
                if AT_XBC <= k < AT_XBC + CM:
                    m = k - AT_XBC
                    f = fill_of("xbc", m)
                    o = begin(g, f)
                    for h in range(CH):
                        mm = e.matmul(o[:, :], inT_sb[:, h, C + m * P:C + (m + 1) * P], uT[:, h, :],
                                      start=(h == 0), stop=(h == CH - 1))
                    mm.then_inc(filled, 1)
                if AT_Z <= k < AT_Z + 2:
                    r = k - AT_Z
                    f = fill_of("z", r)
                    o = begin(g, f)
                    for t in range(2):
                        for h in range(CH):
                            mm = e.matmul(o[:, t * C:(t + 1) * C], uT[:, h, (2 * r + t) * P:(2 * r + t + 1) * P],
                                          inT_sb[:, h, 0:C], start=(h == 0), stop=(h == CH - 1))
                    mm.then_inc(filled, 1)
                if k == AT_DAT:
                    f = fill_of("dAT")
                    o = begin(g, f)
                    e.wait_ge(dA_done, g + 2)
                    e.transpose(o[0:TH, 0:P], dA16[:, :], ident[:, :]).then_inc(filled, 1)
                if k == AT_CUM:
                    f = fill_of("cumT")
                    o = begin(g, f)
                    e.wait_ge(cum_ready, g + 2)
                    settle(e)
                    e.transpose(o[:, 0:TH], cumr[:, :], ident[0:TH, 0:TH]).then_inc(filled, 1)
                if AT_XSB <= k < AT_XSB + 2:
                    for c in range(2 * (k - AT_XSB), 2 * (k - AT_XSB) + 2):
                        f = fill_of("xsB", c)
                        o = begin(g, f)
                        e.wait_ge(silu_done, (g + 1) * CM + 1)
                        for m in range(CM - 1):
                            mm = e.transpose(o[:, m * P:(m + 1) * P], xc[:, m, c * P:(c + 1) * P], ident[:, :])
                        mm.then_inc(filled, 1)
                for c in range(QT):
                    if k == AT_CHUNK + CHUNK_STEPS * c + 2:
                        f = fill_of("y", c)
                        o = begin(g, f)
                        e.wait_ge(act_emptied, n_emptied(g, fill_of("xsB", c)))
                        e.wait_ge(state_zero, zero_count(g) + 1)
                        e.wait_ge(S_ready, g * QT + c + 1)
                        e.matmul(o[:, C:2 * C], xc[:, 3, c * P:(c + 1) * P], S[:, :], start=True, stop=True)
                        e.wait_ge(mt_ready, g * QT + c + 2)
                        for h in range(NH):
                            mm = e.matmul(o[:, h * HD:(h + 1) * HD], mt[:, h, :], xsB[:, c, h * HD:(h + 1) * HD],
                                          start=True, stop=True)
                        mm.then_inc(filled, 1)
                        f = fill_of("st", c)
                        o = begin(g, f)
                        e.wait_ge(xw_ready, g * QT + c + 2)
                        e.matmul(o[:, 0:C], xsB[:, c, C:C + NST], xw[:, :], start=True, stop=True).then_inc(filled, 1)
                if k == AT_YT:
                    e.wait_ge(yn_ready, g + 2)
                    for h in range(CH):
                        turn(g, fill_of("yT", h), x1, h)
                if k == AT_OUT:
                    e.wait_ge(act_emptied, n_emptied(g, fill_of("yT", 1)))
                    for m in range(CH):
                        f = fill_of("out", m)
                        o = begin(g, f)
                        for h in range(CH):
                            mm = e.matmul(o[:, :], outT_sb[:, h, m * P:(m + 1) * P], yT[:, h, :],
                                          start=(h == 0), stop=(h == CH - 1))
                        mm.then_inc(filled, 1)

            with e.Fori(0, B) as b:
                projections(b)
                e.wait_ge(k_loaded, (b + 1) * 48 + 1)
                for n in range(KT):
                    max_tile(b * NB, n, acc)
                max_rows(b * NB)
                first_energies(b * NB)
                energies(b * NB, 1)

                def zero_count(g):
                    return b + 1

                attention(b * NB, True, False)
                with e.Fori(1, NB - 1) as i:
                    attention(b * NB + i, True, True)
                attention(b * NB + NB - 1, False, True)
                for k in range(KT):
                    layer1_early(b * NB + NB - 1, k)
                    layer1(b * NB + NB - 1, k)
                e.wait_ge(pooled_ready, b + 2)
                e.wait_ge(act_emptied, (b + 1) * NB * PER_EMPTIER[0] + 1)
                for h in range(CH):
                    mm = e.matmul(pl[0][0:C // 4, 0:1], se1T_sb[:, h, :], pools[:, h:h + 1],
                                  start=(h == 0), stop=(h == CH - 1))
                mm.then_inc(se1_filled, 1)
                e.wait_ge(hdn_ready, b + 2)
                for h in range(CH):
                    mm = e.matmul(pl[1][:, h:h + 1], se2T_sb[:, h * P:(h + 1) * P], hdn[:, :],
                                  start=True, stop=True)
                mm.then_inc(se2_filled, 1)

        @block.vector
        def _(e):
            v = nc.vector
            v.memset(v_hi[:, :, :], 1.0)
            v.memset(v_lo[:, :, :], 0.0)
            e.wait_ge(consts_ready, 2)
            v.tensor_reduce(wmax[:, 0:1], wnat[:, 0:2 * C], AX.X, ALU.max, apply_absolute_value=True)
            v.tensor_reduce(wmax[:, 1:2], wnat[:, 2 * C:3 * C], AX.X, ALU.max, apply_absolute_value=True)
            v.tensor_reduce(wmax[:, 2:3], wnat[:, 3 * C:4 * C], AX.X, ALU.max, apply_absolute_value=True)
            v.tensor_scalar(alog[:, :], alog[:, :], 80.0, None, ALU.min)
            v.tensor_scalar(gbv[:, :], bvcol, gam[:, 0:1], None, ALU.mult)
            v.tensor_scalar(cw[:, :, :], cw[:, :, :], 0.5, None, ALU.mult)
            v.tensor_scalar(cb[:, :], cb[:, :], 0.5, None, ALU.mult)
            e.drain().then_inc(wmax_ready, 1)
            e.wait_ge(prep_done, 2)
            v.tensor_scalar(arow[:, :], arow[:, :], -1.0, None, ALU.mult)
            e.wait_ge(wmax_all, 2)
            e.drain()
            e.sem_inc(lo_done, P32S)

            def scales(b):
                for n in range(CH * 2):
                    h, cut = n // 2, slice((n % 2) * (N // 2), (n % 2 + 1) * (N // 2))
                    e.wait_ge(x_loaded[n], (b + 1) * 16 + 1)
                    v.tensor_reduce(xmax[:, n:n + 1], x_sb[:, h, cut], AX.X, ALU.max, apply_absolute_value=True)
                e.drain().then_inc(xmax_ready, 1)
                e.wait_ge(xmax_all, b + 2)
                v.tensor_reduce(sc[:, 1:2], xmaxa[:, :], AX.X, ALU.max)
                e.drain()
                v.tensor_scalar(sc[:, 1:2], sc[:, 1:2], float(C), None, ALU.mult)
                e.drain()
                v.tensor_scalar(sc[:, 2:5], wmaxa[:, 0:3], sc[:, 1:2], 1e-30, ALU.mult, ALU.max)
                e.drain()
                v.tensor_tensor(sc[:, 3:5], sc[:, 3:5], wmaxa[:, 3:5], ALU.add)
                e.drain()
                v.tensor_scalar(sci[:, 2:5], sc[:, 2:5].bitcast(I32), EXPMASK, None, ALU.bitwise_and)
                e.drain()
                v.tensor_scalar(sc[:, 0:1].bitcast(I32), sci[:, 2:3], -1.0, float((2 * 127 + 14) << 23),
                                ALU.mult, ALU.add)
                v.tensor_tensor(sci[:, 5:6], sci[:, 4:5], sci[:, 3:4], ALU.subtract)
                e.drain()
                v.tensor_scalar(sci[:, 6:7], sci[:, 5:6], 0.5, float(ONEBITS), ALU.mult, ALU.add)
                e.drain()
                v.tensor_scalar(sci[:, 7:8], sci[:, 6:7], EXPMASK, None, ALU.bitwise_and)
                e.drain()
                v.tensor_copy(qkscale[0:D, :].bitcast(I32), sci[0:D, 7:8])
                v.tensor_scalar(qkscale[D:2 * D, :].bitcast(I32), sci[D:2 * D, 7:8], -1.0, float(2 * ONEBITS),
                                ALU.mult, ALU.add)
                v.reciprocal(sc[:, 6:7], sc[:, 0:1])
                e.drain()
                v.tensor_tensor(sc[:, 7:8], sc[:, 6:7], gam[:, :], ALU.mult)
                e.drain().then_inc(scales_ready, 1)

            def split_projections(b):
                e.wait_ge(k_loaded, b * 48 + 1)
                e.wait_ge(q_loaded, b * NB * 48 + 1)
                e.wait_ge(pv_done, b * NB * KT + RING + 1)
                settle(e)
                with e.Fori(0, NB) as j:
                    e.wait_ge(qk_filled, b * NB + j + 2)
                    v.tensor_scalar(qkf[:, :], p_et[0:2 * D, :], bqk_sb[:, :], qkscale[:, :], ALU.add, ALU.mult)
                    e.drain()
                    e.wait_ge(qk_stored, b * NB * 32 + j * 32 + 1)
                    v.tensor_copy(qk_hi[:, :], qkf[:, :])
                    e.drain()
                    v.tensor_tensor(qk_lo[:, :], qkf[:, :], qk_hi[:, :],
                                    ALU.subtract).then_inc(qk_emptied, 1)
                    for t in range(2):
                        e.wait_ge(v_hi_done, b * NB * 2 + j * 2 + t + 2)
                        settle(e)
                        v.scalar_tensor_tensor(v_lo[:, bass.ds(j * 4 + t * 2, 2), 0:C],
                                               pl[t][:, :].rearrange("p (n c) -> p n c", n=2), sc[:, 0:1],
                                               v_hi[:, bass.ds(j * 4 + t * 2, 2), 0:C],
                                               ALU.mult, ALU.subtract).then_inc(v_lo_done, 1)

            def max_tile(g, n, banks):
                e.wait_ge(mx_ready, g * KT + n + 2)
                v.tensor_reduce(maxes[:, n // KB, n % KB:n % KB + 1], banks[n % len(banks)][:, :], AX.X, ALU.max)\
                    .then_inc(max_done, 1)

            def max_parts(g):
                e.drain()
                v.tensor_reduce(mcol[:, 0, :], maxes[:, :, :], AX.X, ALU.max)
                e.drain()
                v.tensor_scalar(mcol[:, 1, :], mcol[:, 0, :], -PSHIFT, 1.0 / MROW, ALU.add, ALU.mult)
                e.drain()
                v.tensor_copy(mparts[:, :, 0], mcol[:, 1, :])
                e.drain()
                v.tensor_tensor(mparts[:, :, 1], mcol[:, 1, :], mparts[:, :, 0], ALU.subtract)\
                    .then_inc(m_ready, 1)

            def next_queries(g):
                e.wait_ge(m_filled, g + 2)
                v.tensor_copy(q_next[STK:STK + 2, :], p_mx[STK:STK + 2, :]).then_inc(q_next_done, 1)
                e.wait_ge(et_ready, g * KT + 1)
                e.wait_ge(q_next_done, g + 2)
                v.tensor_copy(q_cur[:, :], q_next[:, :]).then_inc(q_cur_ready, 1)

            def lo_tile(g, k, behind):
                if behind and k in POOL_LOW:
                    return
                e.wait_ge(hi_done, g * KT + k + 2)
                e.wait_ge(pv_done, g * KT + k + 2)
                if behind and k - 1 in POOL_LOW:
                    e.wait_ge(lo_done, g * KT + k + P32S + 1)
                v.tensor_tensor(p_lo[:, k % RING, :], p32[:, k % P32S, :], p_hi[:, k % RING, :],
                                ALU.subtract).then_inc(lo_done, 1)

            def attention(g, more, behind):
                lo_tile(g, 0, behind)
                if behind:
                    output0(g - 1)
                for k in range(KT):
                    if more:
                        for n in MAX_TILES[k][:1]:
                            max_tile(g + 1, n, [p_mx])
                        if k == KT - 1:
                            next_queries(g + 1)
                    if k + 1 < KT:
                        lo_tile(g, k + 1, behind)
                    if more:
                        for n in MAX_TILES[k][1:]:
                            max_tile(g + 1, n, [p_mx])
                        if k == KT - 3:
                            max_parts(g + 1)
                    if behind:
                        layer1(g - 1, k)

            def rsqrt_guess(src, scale, eps):
                v.tensor_scalar(nw[:, 0, :], src, scale, eps, ALU.mult, ALU.add)
                e.drain()
                v.tensor_scalar(nwi[:, 1, :], nwi[:, 0, :], 1, None, ALU.logical_shift_right)
                v.tensor_scalar(nw[:, 2, :], nw[:, 0, :], -0.5, None, ALU.mult)
                e.drain()
                v.tensor_scalar(nwi[:, 3, :], nwi[:, 1, :], -1.0, float(0x5F3759DF), ALU.mult, ALU.add)

            def newton(steps):
                for _ in range(steps):
                    e.drain()
                    v.tensor_tensor(nw[:, 0, :], nw[:, 3, :], nw[:, 3, :], ALU.mult)
                    e.drain()
                    v.tensor_tensor(nw[:, 1, :], nw[:, 0, :], nw[:, 2, :], ALU.mult)
                    e.drain()
                    v.scalar_tensor_tensor(nw[:, 3, :], nw[:, 1, :], 1.5, nw[:, 3, :], ALU.add, ALU.mult)
                e.drain()

            def output0(g):
                e.wait_ge(pv_done, (g + 1) * KT + RING + 1)
                e.wait_ge(act_emptied, n_emptied(g, fill_of("xT", 1)))
                for t in range(QT):
                    v.reciprocal(rden[:, 0, t:t + 1], acc[t][:, C:C + 1])
                e.drain()
                v.tensor_scalar(rden[:, 1, :], rden[:, 0, :], sc[:, 7:8], None, ALU.mult)
                e.drain()
                for t in range(QT):
                    v.scalar_tensor_tensor(x1[:, t, :], acc[t][:, 0:C], rden[:, 1, t:t + 1], xT[:, t, :],
                                           ALU.mult, ALU.add).then_inc(x1_done, 1)

            def layer1(g, k):
                if k == AT_NORM:
                    e.drain()
                    for t in range(QT):
                        v.bn_stats(bst[:, t, :], x1[:, t, :])
                    e.drain()
                    for t in range(QT):
                        v.bn_aggr(mv[:, t, :], bst[:, t, :])
                    e.drain()
                if k == AT_NORM + 1:
                    rsqrt_guess(mv[:, :, 1], 1.0, 1e-5)
                    newton(2)
                if k == AT_NORM + 2:
                    newton(2)
                    for t in range(QT):
                        ins = v.tensor_scalar(u[:, t, :], x1[:, t, :], mv[:, t, 0:1], nw[:, 3, t:t + 1],
                                              ALU.subtract, ALU.mult)
                    ins.then_inc(u_ready, 1)
                if k == AT_DT:
                    f = fill_of("dt")
                    e.wait_ge(filled, n_filled(g, f))
                    v.tensor_tensor(dtt[:, 0, :].rearrange("p (t h) -> p t h", h=NH),
                                    bank(f)[:, 0:TH].rearrange("p (t h) -> p t h", h=NH),
                                    dtb[:, :].unsqueeze(1).to_broadcast([P, QT, NH]), ALU.add).then_inc(dve_emptied, 1)
                    e.drain()
                    v.scalar_tensor_tensor(dtt[:, 1, :], dtt[:, 0, :], -1.0, dtt[:, 0, :], ALU.mult, ALU.max)\
                        .then_inc(dtabs_ready, 1)
                    v.tensor_scalar(dtt[:, 3, :], dtt[:, 0, :], 0.0, None, ALU.max)
                if k == AT_XBC:
                    e.wait_ge(dtexp_done, g + 2)
                    v.tensor_scalar(dtt[:, 4, :], dtt[:, 2, :], 2.0, None, ALU.add)
                    e.drain()
                    v.reciprocal(dtt[:, 5, :], dtt[:, 4, :])
                    e.drain()
                    v.tensor_tensor(dtt[:, 4, :], dtt[:, 2, :], dtt[:, 5, :], ALU.mult)
                    e.drain()
                    v.tensor_tensor(dtt[:, 5, :], dtt[:, 4, :], dtt[:, 4, :], ALU.mult)
                    e.drain()
                    v.tensor_scalar(dtt[:, 6, :], dtt[:, 5, :], 1.0 / 17, None, ALU.mult)
                if AT_XBC + 1 <= k < AT_XBC + 3:
                    e.drain()
                    for n in ((15, 13, 11, 9) if k == AT_XBC + 1 else (7, 5, 3)):
                        v.scalar_tensor_tensor(dtt[:, 6, :], dtt[:, 6, :], 1.0 / n, dtt[:, 5, :], ALU.add, ALU.mult)
                        e.drain()
                if k == AT_XBC + 2:
                    v.scalar_tensor_tensor(dtt[:, 6, :], dtt[:, 6, :], 1.0, dtt[:, 4, :], ALU.add, ALU.mult)
                    e.drain()
                    v.scalar_tensor_tensor(dt16[:, :], dtt[:, 6, :], 2.0, dtt[:, 3, :], ALU.mult, ALU.add)
                    e.drain()
                    v.tensor_tensor(dtt[:, 7, :].rearrange("p (t h) -> p t h", h=NH),
                                    dt16[:, :].rearrange("p (t h) -> p t h", h=NH),
                                    arow[:, :].unsqueeze(1).to_broadcast([P, QT, NH]), ALU.mult).then_inc(dt_ready, 1)
                if AT_XBC + 1 <= k < AT_XBC + 1 + CM:
                    m = k - AT_XBC - 1
                    e.wait_ge(tap0_done, g * CM + m + 2)
                    for j in range(HALO - 1, -1, -1):
                        ins = v.scalar_tensor_tensor(acc_c[:, m, :], xbc[:, m, j:j + BLK], cw[:, m, j:j + 1],
                                                     acc_c[:, m, :], ALU.mult, ALU.add)
                        if j:
                            e.drain()
                    ins.then_inc(conv_done, 1)
                if k == AT_XBC + CM:
                    e.drain()
                    v.tensor_copy(xbc[:, :, 0:HALO], xbc[:, :, BLK:BLK + HALO]).then_inc(halo_done, 1)
                if k == AT_DAT:
                    f = fill_of("dAT")
                    e.wait_ge(filled, n_filled(g, f))
                    e.wait_ge(rows_stored, g * 32 + 1)
                    v.tensor_copy(dAr[:, :], bank(f)[0:TH, 0:P]).then_inc(dve_emptied, 1)
                    e.drain()
                    v.tensor_tensor_scan(cumr[:, :], dAr[:, :], zrow[:, :], 1.0, ALU.mult, ALU.add)\
                        .then_inc(cum_ready, 1)
                    e.drain()
                    v.memset(dAr[:, 0:1], 0.0).then_inc(rows_ready, 1)
                if k == AT_CUM:
                    f = fill_of("cumT")
                    e.wait_ge(filled, n_filled(g, f))
                    v.tensor_copy(cum16[:, :], bank(f)[:, 0:TH]).then_inc(dve_emptied, 1)
                if AT_XBC + 3 <= k < AT_XBC + 3 + CM:
                    m = k - AT_XBC - 3
                    e.wait_ge(tanh_done, g * CM + m + 2)
                    v.scalar_tensor_tensor(xc[:, m, :], th[:, m % 2, :], 1.0, acc_c[:, m, :], ALU.add, ALU.mult)\
                        .then_inc(silu_done, 1)
                if k == AT_Z + 2:
                    e.wait_ge(zt_done, g + 2)
                    v.scalar_tensor_tensor(zt[:, :, :], zt[:, :, :], 1.0, zh[:, :, :], ALU.add, ALU.mult)\
                        .then_inc(zs_done, 1)
                for c in range(QT):
                    if k == AT_CHUNK + CHUNK_STEPS * (c + 1):
                        f = fill_of("y", c)
                        e.wait_ge(filled, n_filled(g, f))
                        e.wait_ge(xd_ready, g * QT + c + 2)
                        e.wait_ge(y_ready, g * QT + c + 1)
                        v.tensor_tensor(yt[:, 0, :], bank(f)[:, 0:C], xd[:, :], ALU.add)
                        v.tensor_tensor(yt[:, 1, :].rearrange("p (h d) -> p h d", h=NH),
                                        bank(f)[:, C:2 * C].rearrange("p (h d) -> p h d", h=NH),
                                        cum16[:, c * NH:(c + 1) * NH].unsqueeze(2).to_broadcast([P, NH, HD]),
                                        ALU.mult).then_inc(y1_ready, 1)
                        e.drain().then_inc(dve_emptied, 1)
                        f = fill_of("st", c)
                        e.wait_ge(filled, n_filled(g, f))
                        e.wait_ge(Sd_ready, g * QT + c + 2)
                        v.tensor_tensor(S[:, :], bank(f)[:, 0:C], Sd[:, :], ALU.add).then_inc(S_ready, 1)
                        e.drain().then_inc(dve_emptied, 1)
                    if k == AT_CHUNK + CHUNK_STEPS * c:
                        e.wait_ge(rows_loaded, (g + 1) * 32 + 1)
                        e.wait_ge(idt_ready, g * QT + c + 2)
                        e.wait_ge(xw_ready, g * QT + c + 1)
                        v.tensor_tensor_scan(lt[:, :, :].rearrange("p h i -> p (h i)"),
                                             dAb[:, c * NH * P:(c + 1) * NH * P],
                                             idt[:, c % 2].rearrange("p h i -> p (h i)"), 0.0, ALU.mult, ALU.add)\
                            .then_inc(scan_done, 1)
                        e.drain().then_inc(lt_ready, 1)
                    if k == AT_CHUNK + CHUNK_STEPS * c + 1:
                        f = fill_of("cb", c)
                        e.wait_ge(filled, n_filled(g, f))
                        v.tensor_tensor(mt[:, :, :], bank(f)[:, 0:P].unsqueeze(1).to_broadcast([P, NH, P]),
                                        lt[:, :, :], ALU.mult).then_inc(mt_ready, 1)
                        e.drain().then_inc(dve_emptied, 1)
                if k == AT_RMS:
                    e.wait_ge(sq_done, (g + 1) * QT + 1)
                    rsqrt_guess(ms[:, :], 1.0 / C, 1e-5)
                    newton(2)
                if k == AT_RMS + 1:
                    newton(2)
                    for t in range(QT):
                        ins = v.tensor_scalar(x1[:, t, :], y[:, t, :], nw[:, 3, t:t + 1], None, ALU.mult)
                    ins.then_inc(yn_ready, 1)
                if k == AT_OUT + 1:
                    e.wait_ge(act_emptied, n_emptied(g, fill_of("out", 1)))
                    v.tensor_tensor(pools[:, :], pools[:, :], pool1[:, :], ALU.add).then_inc(pool_done, 1)

            v.memset(zrow[:, :], 0.0)
            e.drain()
            with e.Fori(0, B) as b:
                scales(b)
                v.memset(pools[:, :], 0.0)
                v.memset(xbc[:, :, 0:HALO], 0.0).then_inc(halo_done, 1)
                split_projections(b)
                for n in range(KT):
                    max_tile(b * NB, n, acc)
                max_parts(b * NB)
                next_queries(b * NB)
                attention(b * NB, True, False)
                with e.Fori(1, NB - 1) as i:
                    attention(b * NB + i, True, True)
                attention(b * NB + NB - 1, False, True)
                output0(b * NB + NB - 1)
                for k in range(KT):
                    layer1(b * NB + NB - 1, k)
                e.drain()
                v.tensor_scalar(pools[:, :], pools[:, :], 1.0 / N, None, ALU.mult).then_inc(pooled_ready, 1)
                e.wait_ge(gate_th, b + 2)
                v.tensor_scalar(gate[:, :], gate[:, :], 0.5, 0.5, ALU.mult, ALU.add)
                e.drain()
                for n in range(CH * 2):
                    h, cut = n // 2, slice((n % 2) * (N // 2), (n % 2 + 1) * (N // 2))
                    v.scalar_tensor_tensor(img[:, h, cut], img[:, h, cut], gate[:, h:h + 1], x_sb[:, h, cut],
                                           ALU.mult, ALU.add).then_inc(final_done, 1)


def kernel(**inputs):
    import numpy as _np
    import concourse.bacc as _bacc
    from concourse import mybir as _mybir
    from concourse.bass_utils import run_bass_kernel_spmd as _run

    a = {k: _np.asarray(v) for k, v in inputs.items()}
    x = a["x"]
    wqk = _np.concatenate([a["L0_conv_wq"], a["L0_conv_wk"]], 0)
    arrs = {
        "x": x.reshape(x.shape[0], x.shape[1], -1),
        "wqkT": wqk.T, "bqk": _np.concatenate([a["L0_conv_bq"], a["L0_conv_bk"]]),
        "wvT": a["L0_conv_wv"].T, "wv": a["L0_conv_wv"], "gamma": a["L0_conv_gamma"],
        "inT": a["L1_conv_in_w"].T, "wqk": wqk,
        "conv_w": a["L1_conv_conv_w"], "conv_b": a["L1_conv_conv_b"].reshape(-1, P).T,
        "dt_bias": a["L1_conv_dt_bias"], "A_log": a["L1_conv_A_log"], "Dp": a["L1_conv_Dp"],
        "outT": a["L1_conv_out_w"].T, "se1T": a["L1_conv_se1_w"].T, "se1_b": a["L1_conv_se1_b"],
        "se2T": a["L1_conv_se2_w"].T,
        "columns": _np.stack([a[k].reshape(-1, P) for k in ("L1_conv_norm_g", "L1_conv_norm_b", "L1_conv_rms_w",
                                                            "L0_conv_bv", "L1_conv_se2_b")], 0).transpose(2, 0, 1),
    }
    nc = _bacc.Bacc("TRN2", target_bir_lowering=False, num_devices=1)
    arrays, args = {}, []
    for name, v in arrs.items():
        v = _np.ascontiguousarray(v)
        arrays[f"in_{name}_dram"] = v
        args.append(nc.dram_tensor(f"in_{name}_dram", v.shape, _mybir.dt.from_np(v.dtype), kind="ExternalInput").ap())
    shape = arrs["x"].shape
    args.append(nc.dram_tensor("out_0_dram", shape, _mybir.dt.float32, kind="ExternalOutput").ap())
    conv_attention_mamba_kernel(nc, *args)
    r = _run(nc, [arrays], core_ids=[0])
    return r.results[0]["out_0_dram"].reshape(x.shape)
```
